# Optimizing a Trainium2 kernel written in Bass

```python
import numpy as np
import jax
import jax.numpy as jnp

def _softmax(x, axis=-1):
    return jax.nn.softmax(x, axis=axis)

def _gelu(x):
    return jax.nn.gelu(x, approximate=True)

def _silu(x):
    return jax.nn.silu(x)

def _sigmoid(x):
    return jax.nn.sigmoid(x)

def _layernorm(x, axis=-1, eps=1e-05):
    m = jnp.mean(x, axis=axis, keepdims=True)
    v = jnp.var(x, axis=axis, keepdims=True)
    return (x - m) / jnp.sqrt(v + eps)

def _scatter_add(tgt, idx, src, axis=0):
    return tgt.at[idx].add(src)

def _segment_sum(src, seg, n):
    return jax.ops.segment_sum(src, seg, n)
kernel_name = 'mk_adj_ffn_d1_adj_r2_2ec9cd'

def setup_inputs(seed: int=0):
    np.random.seed(seed)
    _w = jnp.asarray

    def _rec_inputs():
        import jax
        import jax.numpy as jnp
        _gk = jax.random.key(seed)
        x = -0.0005207 + 1.001 * jax.random.normal(jax.random.fold_in(_gk, 1), (4096, 128), jnp.float32)
        _w = (1.0 + jnp.arange(4096, dtype=jnp.float32)) ** (-0.5)
        _w = _w / _w.mean()
        _pij = jnp.clip(0.000976562 * _w[:, None] * _w[None, :], 0.0, 1.0)
        _a = jax.random.uniform(jax.random.fold_in(_gk, 2), (4096, 4096)) < _pij
        adj = _a.astype(jnp.int32)
        return (x, adj)
    x, adj = _rec_inputs()

    def _L0_gnn_setup():
        import jax, jax.numpy as jnp
        import numpy as np
        N, D, H = (4096, 128, 128)
        NEG_BIG = -1000000000.0
        LEAKY_SLOPE = 0.01
        key = jax.random.key(seed)
        ks = jax.random.split(key, 6)
        inlayer = jax.random.normal(ks[0], (N, D), jnp.float32)
        inlayer2 = jax.random.normal(ks[1], (N, D), jnp.float32)
        adj_mat = jax.random.randint(ks[2], (N, N), 0, 2, jnp.int32)
        W = jax.random.uniform(ks[3], (H, D), jnp.float32, -1.0, 1.0) * np.float32(np.sqrt(6.0 / (D + H)))
        b = jnp.zeros((H,), jnp.float32)
        w1 = jax.random.uniform(ks[4], (H,), jnp.float32, -1.0, 1.0) * np.float32(np.sqrt(6.0 / (H + 1)))
        b1 = jnp.zeros((1,), jnp.float32)
        w2 = jax.random.uniform(ks[5], (H,), jnp.float32, -1.0, 1.0) * np.float32(np.sqrt(6.0 / (H + 1)))
        b2 = jnp.zeros((1,), jnp.float32)
        return {'inlayer': inlayer, 'inlayer2': inlayer2, 'adj_mat': adj_mat, 'W': W, 'b': b, 'w1': w1, 'b1': b1, 'w2': w2, 'b2': b2}
    _L0_gnn_all = _L0_gnn_setup()
    _L0_gnn_in = {k: v for k, v in _L0_gnn_all.items() if k in ('inlayer2', 'W', 'b', 'w1', 'b1', 'w2', 'b2')}
    del _L0_gnn_all

    def _L0_ffn_setup():
        import jax, jax.numpy as jnp
        import numpy as np
        B, T, D, H, E = (16, 2048, 128, 256, 8)
        key = jax.random.key(seed)
        ks = jax.random.split(key, 5)
        x = jax.random.normal(ks[0], (B, T, D), dtype=jnp.float32)
        gate_w = jax.random.normal(ks[1], (D, E), dtype=jnp.float32) * 0.02
        gate_b = jnp.zeros((E,), dtype=jnp.float32)
        W1 = jax.random.normal(ks[2], (E, D, H), dtype=jnp.float32) * 0.02
        b1 = jnp.zeros((E, H), dtype=jnp.float32)
        W2 = jax.random.normal(ks[3], (E, H, D), dtype=jnp.float32) * 0.02
        b2 = jnp.zeros((E, D), dtype=jnp.float32)
        return {'x': x, 'gate_w': gate_w, 'gate_b': gate_b, 'W1': W1, 'b1': b1, 'W2': W2, 'b2': b2}
    _L0_ffn_all = _L0_ffn_setup()
    _L0_ffn_in = {k: v for k, v in _L0_ffn_all.items() if k in ('gate_w', 'gate_b', 'W1', 'b1', 'W2', 'b2')}
    del _L0_ffn_all
    return {'x': x, 'adj': adj, 'L0_gnn_inlayer2': _L0_gnn_in['inlayer2'], 'L0_gnn_W': _L0_gnn_in['W'], 'L0_gnn_b': _L0_gnn_in['b'], 'L0_gnn_w1': _L0_gnn_in['w1'], 'L0_gnn_b1': _L0_gnn_in['b1'], 'L0_gnn_w2': _L0_gnn_in['w2'], 'L0_gnn_b2': _L0_gnn_in['b2'], 'L0_ffn_gate_w': _L0_ffn_in['gate_w'], 'L0_ffn_gate_b': _L0_ffn_in['gate_b'], 'L0_ffn_W1': _L0_ffn_in['W1'], 'L0_ffn_b1': _L0_ffn_in['b1'], 'L0_ffn_W2': _L0_ffn_in['W2'], 'L0_ffn_b2': _L0_ffn_in['b2']}

def reference(x, adj, L0_gnn_inlayer2, L0_gnn_W, L0_gnn_b, L0_gnn_w1, L0_gnn_b1, L0_gnn_w2, L0_gnn_b2, L0_ffn_gate_w, L0_ffn_gate_b, L0_ffn_W1, L0_ffn_b1, L0_ffn_W2, L0_ffn_b2):
    import jax
    import jax.numpy as jnp

    def _L0_gnn_ref(inlayer, inlayer2, adj_mat, W, b, w1, b1, w2, b2):
        import jax, jax.numpy as jnp
        import numpy as np
        N, D, H = (4096, 128, 128)
        NEG_BIG = -1000000000.0
        LEAKY_SLOPE = 0.01
        h = inlayer2 @ W.T + b
        f1 = h @ w1 + b1
        f2 = h @ w2 + b2
        logits = f1[:, None] + f2[None, :]
        bias_mat = NEG_BIG * (1.0 - (adj_mat > 0).astype(jnp.float32))
        coefs = jax.nn.softmax(jax.nn.leaky_relu(logits, LEAKY_SLOPE) + bias_mat, axis=-1)
        vals = coefs @ inlayer
        return vals

    def _L0_ffn_ref(x, gate_w, gate_b, W1, b1, W2, b2):
        import jax, jax.numpy as jnp
        import numpy as np
        B, T, D, H, E = (16, 2048, 128, 256, 8)
        Bb, Tt, Dd = x.shape
        Ee = gate_w.shape[1]
        xf = x.reshape(-1, Dd)
        N = xf.shape[0]
        logits = xf @ gate_w + gate_b
        probs = jax.nn.softmax(logits, axis=-1)
        top2_vals, top2_idx = jax.lax.top_k(probs, 2)
        cw = jnp.zeros((N, Ee), dtype=xf.dtype).at[jnp.arange(N)[:, None], top2_idx].add(top2_vals)

        def step(acc, params):
            w1, bb1, w2, bb2, we = params
            h = jax.nn.gelu(xf @ w1 + bb1, approximate=False)
            y = h @ w2 + bb2
            return (acc + we[:, None] * y, None)
        out, _ = jax.lax.scan(step, jnp.zeros_like(xf), (W1, b1, W2, b2, cw.T))
        return out.reshape(Bb, Tt, Dd)
    x = x + _L0_gnn_ref(_layernorm(x, axis=-1), L0_gnn_inlayer2, adj, L0_gnn_W, L0_gnn_b, L0_gnn_w1, L0_gnn_b1, L0_gnn_w2, L0_gnn_b2)
    x = x + _L0_ffn_ref(_layernorm(x, axis=-1)[None], L0_ffn_gate_w, L0_ffn_gate_b, L0_ffn_W1, L0_ffn_b1, L0_ffn_W2, L0_ffn_b2)[0]
    return x

_drawn_inputs = setup_inputs


def setup_inputs(seed=0):
    import zlib

    import numpy as np

    out = dict(_drawn_inputs(seed))
    spreads = {'L0_gnn_b': (0.0, 0.1),
     'L0_ffn_gate_b': (0.0, 0.585),
     'L0_ffn_b1': (0.0, 0.8),
     'L0_ffn_b2': (0.0, 0.436)}
    factors = {'L0_ffn_gate_w': 3.314, 'L0_ffn_W1': 7.767, 'L0_ffn_W2': 7.089}
    for name, (base, spread) in spreads.items():
        noise = np.random.default_rng([zlib.crc32(name.encode()), seed]).standard_normal(out[name].shape)
        drawn = base * np.exp(spread * noise) if base else spread * noise
        out[name] = jnp.asarray(drawn.astype(out[name].dtype))
    for name, factor in factors.items():
        out[name] = (out[name] * factor).astype(out[name].dtype)
    return out
```

```python
from contextlib import ExitStack

import concourse.bass as bass
from concourse import mybir

P = 128
ALU = mybir.AluOpType
ACT = mybir.ActivationFunctionType
F32 = mybir.dt.float32
F16 = mybir.dt.float16
U8 = mybir.dt.uint8
U32 = mybir.dt.uint32
I32 = mybir.dt.int32
AX_X = mybir.AxisListType.X
RMAX = bass.bass_isa.ReduceOp.max

SLOPE = 0.01
STEEP = 1.0 - SLOPE
LN_EPS = 1e-5

X_SCALE = 1024.0
W_SCALE = 256.0
C_SCALE = 64.0


def gnn_moe_kernel(nc, x, adj, in2, gnn_w, gnn_b, gnn_w1, gnn_b1, gnn_w2, gnn_b2,
                   gate_w, gate_b, W1, b1, W2, b2, out):
    N, D = x.shape
    E, _, H = W1.shape
    NK = N // P
    ST = 512
    NS = N // ST
    TS = ST // P
    Q = 4
    QJ = N // Q
    NB = QJ // P
    PR = 64
    NP = ST // PR
    PS_ = PR // 32
    SLOTS = 4
    CR = 4
    FC = H // P
    LAG = 3
    assert D == P and NS % 2 == 0 and E % 4 == 0 and FC == 2 and NP == 2 * SLOTS

    with ExitStack() as ctx:
        def sb(name, shape, dt=F32):
            return ctx.enter_context(nc.sbuf_tensor(name, shape, dt))

        def sem(name):
            return ctx.enter_context(nc.semaphore(name))

        bank = ctx.enter_context(nc.psum_tensor("bank", [P, 8, 512], F32))

        stage = sb("stage", [P, SLOTS, PS_, QJ], I32)
        maskT = sb("maskT", [P, 2, ST // 32, NB, 32, 4], U8)
        mask = sb("mask", [P, 2, PS_, QJ], U8)
        g_row = sb("g_row", [P, N])
        Y = sb("Y", [P, NK, D])
        x2 = sb("x2", [P, NK, D])
        share1 = sb("share1", [P, N])
        share2 = sb("share2", [P, N])
        share3 = sb("share3", [P, N])
        c = sb("c", [P, CR, ST])
        w1h = sb("w1h", [P, E, H], F16)
        w1l = sb("w1l", [P, E, H], F16)
        w2h = sb("w2h", [P, E * FC, D], F16)
        w2l = sb("w2l", [P, E * FC, D], F16)

        in2_j = share1[:, :].rearrange("p (k d) -> p k d", d=D)
        xin = in2_j
        xnT = share1[:, :]
        in2T = share2[:, :]
        xh = share2[:, 0:N // 2].bitcast(F16)
        xl = share2[:, N // 2:N].bitcast(F16)
        x_j = share3[:, :].rearrange("p (k d) -> p k d", d=D)
        w1raw = share3[:, 0:E * H].rearrange("p (e f) -> p e f", e=E)
        w2raw = share3[:, E * H:2 * E * H].rearrange("p (c d) -> p c d", d=D)

        ones = sb("ones", [P, P])
        ident = sb("ident", [P, P])
        ident16 = sb("ident16", [P, P], F16)
        back = sb("back", [P, D + 2])
        W_sb = sb("W_sb", [P, D])
        w_col = sb("w_col", [P, 2])
        b_col = sb("b_col", [P, 1])
        b_rep = sb("b_rep", [P, P])
        gb12 = sb("gb12", [P, 2])
        c12 = sb("c12", [P, 2])
        G = sb("G", [P, 2])
        g1_rep = sb("g1_rep", [P, P])
        f_sb = sb("f_sb", [P, NK, 2])
        nf2 = sb("nf2", [P, NK])
        part_max = sb("part_max", [P, 3])
        all_max = sb("all_max", [P, 3])
        tmp = sb("tmp", [P, 8])
        bias_g = sb("bias_g", [P, 1])
        bias_r = sb("bias_r", [P, 1])
        bias_u = sb("bias_u", [P, 1])
        eps = sb("eps", [P, 1])
        sig_bias = sb("sig_bias", [P, 1])
        r_col = sb("r_col", [P, NK])
        u_col = sb("u_col", [P, NK])
        ru = sb("ru", [P, NK])
        st1 = sb("st1", [P, NK, 6])
        mv1 = sb("mv1", [P, NK, 2])
        sd1 = sb("sd1", [P, NK])
        rs1 = sb("rs1", [P, NK])
        all_rows = sb("all_rows", [P, D + 1])
        oT = sb("oT", [P, ST])
        fin = sb("fin", [P, TS, D + 1])
        empty = sb("empty", [P, TS])
        rinv = sb("rinv", [P, TS])
        st2 = sb("st2", [P, TS, 6])
        mv2 = sb("mv2", [P, TS, 2])
        sd2 = sb("sd2", [P, TS])
        rs2 = sb("rs2", [P, TS])
        xn2 = sb("xn2", [P, TS, D])
        xs = sb("xs", [P, TS, D])
        diff = sb("diff", [P, TS])
        gate_sb = sb("gate_sb", [P, E])
        gateb_sb = sb("gateb_sb", [P, E])
        order = sb("order", [P, E])
        b1_sb = sb("b1_sb", [E * FC, P])
        b1T = sb("b1T", [P, E * FC])
        b2_sb = sb("b2_sb", [2 * E, D])
        b2h = sb("b2h", [2 * E, D], F16)
        b2l = sb("b2l", [2 * E, D], F16)
        sel = sb("sel", [2 * E, E, P], F16)

        stage32 = stage[:].rearrange("p a b c -> p (a b c)").bitcast(F32)
        h = stage32[:, 0:2 * FC * ST].rearrange("p (r f t) -> p r f t", r=2, f=FC)
        hw = stage32[:, 2 * FC * ST:4 * FC * ST].rearrange("p (r f t) -> p r f t", r=2, f=FC)
        at32 = maskT[:].rearrange("p a b c d e -> p (a b c d e)").bitcast(F32)
        HR = 4
        hh = at32[:, 0:HR * FC * ST // 2].bitcast(F16).rearrange("p (r f t) -> p r f t", r=HR, f=FC)
        hl = at32[:, HR * FC * ST // 2:HR * FC * ST].bitcast(F16).rearrange("p (r f t) -> p r f t", r=HR, f=FC)
        gr = g_row[:, :]
        lg = gr[:, 0:256].rearrange("p (n e) -> p n e", e=E)
        pr = gr[:, 256:512].rearrange("p (n e) -> p n e", e=E)
        code = gr[:, 512:768].rearrange("p (n e) -> p n e", e=E)
        sel1 = gr[:, 768:1024].rearrange("p (n e) -> p n e", e=E)
        sel2 = gr[:, 1024:1280].rearrange("p (n e) -> p n e", e=E)
        rowv = gr[:, 1280:1280 + 4 * NK].rearrange("p (v n) -> p v n", v=4)
        cwT = gr[0:2 * E, 1536:1536 + N // 2].bitcast(F16)
        cw16 = gr[:, 3584:3584 + NK * E].bitcast(F16).rearrange("p (n e) -> p n e", e=2 * E)
        y_sb = c[:, 0, :]
        out_sb = c[:, 1, :].rearrange("p (t d) -> p t d", d=D)

        small_in = sem("small_in")
        in2_in = sem("in2_in")
        xj_in = sem("xj_in")
        xn_in = sem("xn_in")
        w_in = sem("w_in")
        adj_in = [sem(f"adj_in{i}") for i in range(SLOTS)]
        pool_const = sem("pool_const")
        pool_step = sem("pool_step")
        dve_const = sem("dve_const")
        brep_done = sem("brep_done")
        gc_done = sem("gc_done")
        g_copied = sem("g_copied")
        in2t_ready = sem("in2t_ready")
        in2t_copied = sem("in2t_copied")
        f_ready = sem("f_ready")
        f_copied = sem("f_copied")
        pmax_ready = sem("pmax_ready")
        amax_ready = sem("amax_ready")
        bias_ready = sem("bias_ready")
        f1row_ready = sem("f1row_ready")
        grow_ready = sem("grow_ready")
        ru_exp = sem("ru_exp")
        mv1_ready = sem("mv1_ready")
        sd1_ready = sem("sd1_ready")
        rs1_ready = sem("rs1_ready")
        xin_sum = sem("xin_sum")
        S_ready = sem("S_ready")
        y_rows = sem("y_rows")
        wsplit = sem("wsplit")
        b1_ready = sem("b1_ready")
        b1_copied = sem("b1_copied")
        dve_step = sem("dve_step")
        conv_done = sem("conv_done")
        turned = sem("turned")
        c_ready = sem("c_ready")
        c_used = sem("c_used")
        oT_copied = sem("oT_copied")
        n_ready = sem("n_ready")
        post_step = sem("post_step")
        mv2_ready = sem("mv2_ready")
        sd2_ready = sem("sd2_ready")
        xn2_ready = sem("xn2_ready")
        xt_ready = sem("xt_ready")
        xt_copied = sem("xt_copied")
        xh_ready = sem("xh_ready")
        xl_ready = sem("xl_ready")
        lg_ready = sem("lg_ready")
        lgd_ready = sem("lgd_ready")
        pr_ready = sem("pr_ready")
        cw_ready = sem("cw_ready")
        cwt_ready = sem("cwt_ready")
        cwt_copied = sem("cwt_copied")
        h_ready = sem("h_ready")
        gelu_done = sem("gelu_done")
        web_ready = sem("web_ready")
        hw_done = sem("hw_done")
        hh_done = sem("hh_done")
        hl_done = sem("hl_done")
        ffn2_done = sem("ffn2_done")
        y_copied = sem("y_copied")
        yt_ready = sem("yt_ready")
        out_added = sem("out_added")
        out_free = sem("out_free")

        def need(eng, s, v):
            if not (isinstance(v, int) and v <= 0):
                eng.wait_ge(s, v)

        def by_chunk(t):
            return t.rearrange("(q b a e) d -> q a b e d", q=Q, b=NB, a=32, e=4)

        adj_v = adj.rearrange("(t s i) (q j) -> t q i s j", s=PS_, i=32, q=Q)
        out_v = out.rearrange("(n t p) d -> n p t d", t=TS, p=P)
        dst_k = lambda t, q: t[32 * q:32 * q + 32].rearrange("a (b e) d -> a b (e d)", e=4)

        NSMALL = 13
        block = ctx.enter_context(nc.Block())

        @block.sync
        def _(sp):
            for q in range(Q):
                sp.dma_start(dst_k(in2_j, q), by_chunk(in2)[q].rearrange("a b e d -> a b (e d)")).then_inc(in2_in, 16)
            for q in range(Q):
                sp.dma_start(dst_k(x_j, q), by_chunk(x)[q].rearrange("a b e d -> a b (e d)")).then_inc(xj_in, 16)

            def load_adj(s, p):
                need(sp, conv_done, s * NP + p - SLOTS + 1)
                for q in range(Q):
                    sp.dma_start(stage[32 * q:32 * q + 32, p % SLOTS], adj_v[s * NP + p, q]).then_inc(adj_in[p % SLOTS], 16)

            for p in range(NP):
                load_adj(0, p)
            sp.wait_ge(y_rows, 1)
            sp.wait_ge(xin_sum, 1)
            sp.dma_start(w1raw, W1.rearrange("e d f -> d e f")).then_inc(w_in, 16)
            sp.dma_start(w2raw, W2.rearrange("e (c f) d -> f (e c) d", c=FC)).then_inc(w_in, 16)
            with sp.Fori(1, NS) as s:
                for p in range(NP):
                    load_adj(s, p)
            with sp.Fori(0, NS) as st:
                sp.wait_ge(out_added, st + 1)
                sp.dma_start(out_v[st], out_sb).then_inc(out_free, 16)
            sp.wait_ge(out_free, 16 * NS + 1)

        @block.gpsimd
        def _(pool):
            pool.memset(ident[:], 0.0).then_inc(pool_step, 1)
            pool.memset(sel[:], 0.0).then_inc(pool_step, 1)
            pool.memset(all_rows[:, D:D + 1], float(N))
            for e in range(E):
                pool.memset(order[:, e:e + 1], float(E - e))
            pool.wait_ge(pool_step, 2)
            pool.affine_select(out=ident[:], in_=ident[:], compare_op=ALU.not_equal, fill=1.0, base=0,
                               pattern=[[-1, P]], channel_multiplier=1).then_inc(pool_step, 1)
            pool.affine_select(out=sel[:], in_=sel[:], compare_op=ALU.not_equal, fill=1.0, base=0,
                               pattern=[[-1, E], [0, P]], channel_multiplier=1).then_inc(pool_step, 1)
            pool.wait_ge(pool_step, 4)
            pool.affine_select(out=sel[:], in_=sel[:], compare_op=ALU.not_equal, fill=1.0, base=-E,
                               pattern=[[-1, E], [0, P]], channel_multiplier=1).then_inc(pool_step, 1)
            pool.tensor_copy(ident16[:], ident[:])
            pool.tensor_copy(back[:, 0:D - 1], ident[:, 0:D - 1])
            pool.tensor_scalar(back[:, D - 1:D], ident[:, D - 1:D], -1.0, None, ALU.add)
            pool.tensor_copy(back[:, D:D + 1], ident[:, D - 1:D]).then_inc(pool_step, 1)
            pool.wait_ge(pool_step, 6)
            pool.drain().then_inc(pool_const, 1)
            pool.wait_ge(pmax_ready, 1)
            pool.partition_all_reduce(all_max[:], part_max[:], P, RMAX).then_inc(amax_ready, 1)
            pool.wait_ge(rs1_ready, 1)
            pool.wait_ge(in2t_ready, NK // 4)
            for k in range(NK):
                ins = pool.tensor_scalar(xin[:, k], x_j[:, k], mv1[:, k, 0:1], rs1[:, k:k + 1],
                                         ALU.subtract, ALU.mult)
            ins.then_inc(pool_step, 1)
            pool.wait_ge(pool_step, 7)
            n, steps = NK // 2, 7
            while n:
                pool.tensor_tensor(xin[:, 0:n], xin[:, 0:n], xin[:, n:2 * n], ALU.add).then_inc(pool_step, 1)
                steps += 1
                pool.wait_ge(pool_step, steps)
                n //= 2
            pool.drain().then_inc(xin_sum, 1)

        @block.scalar
        def _(act):
            small = [(W_sb[:], gnn_w), (w_col[:, 0:1], gnn_w1.rearrange("(p a) -> p a", a=1)),
                     (w_col[:, 1:2], gnn_w2.rearrange("(p a) -> p a", a=1)),
                     (b_col[:], gnn_b.rearrange("(p a) -> p a", a=1)),
                     (gb12[:, 0:1], gnn_b1.rearrange("(p a) -> p a", a=1).partition_broadcast(P)),
                     (gb12[:, 1:2], gnn_b2.rearrange("(p a) -> p a", a=1).partition_broadcast(P)),
                     (gate_sb[:], gate_w), (gateb_sb[:], gate_b.rearrange("(a e) -> a e", a=1).partition_broadcast(P)),
                     (b1_sb[:], b1.rearrange("e (c f) -> (e c) f", c=FC)),
                     (b2_sb[0:E], b2), (b2_sb[E:2 * E], b2)]
            for dst, src in small:
                if len(src.shape) == 3:
                    src = src.rearrange("p a e -> p (a e)")
                act.dma_start(dst, src).then_inc(small_in, 16)
            act.dma_start(x2[:], x.rearrange("(n p) d -> p n d", p=P)).then_inc(xn_in, 16)

            for b in range(NB):
                act.wait_ge(in2t_ready, b + 1)
                act.activation(in2T[:, 512 * b:512 * b + 512], bank[:, 6 + b % 2, :], ACT.Copy).then_inc(in2t_copied, 1)
            act.wait_ge(mv1_ready, 1)
            act.wait_ge(dve_const, 1)
            act.activation(sd1[:], mv1[:, :, 1], ACT.Sqrt, bias=eps[:]).then_inc(sd1_ready, 1)
            act.wait_ge(bias_ready, 1)
            act.activation(r_col[:], f_sb[:, :, 1], ACT.Exp, bias=bias_r[:], scale=-STEEP).then_inc(ru_exp, 1)
            act.activation(u_col[:], f_sb[:, :, 1], ACT.Exp, bias=bias_u[:]).then_inc(ru_exp, 1)
            g_nat = g_row[:, :].rearrange("p (q b a e) -> p b q a e", q=Q, b=NB, a=32, e=4)
            for b in range(NB):
                act.wait_ge(f1row_ready, b + 1)
                act.activation(g_nat[:, b], bank[:, 6 + b % 2, :].rearrange("p (e q a) -> p q a e", e=4, q=Q),
                               ACT.Exp, bias=bias_g[:], scale=STEEP).then_inc(grow_ready, 1)
            act.wait_ge(b1_ready, 1)
            act.activation(b1T[:], bank[:, 4, 0:E * FC], ACT.Copy).then_inc(b1_copied, 1)

            def convert(s, p):
                act.wait_ge(adj_in[p % SLOTS], 64 * (s * 2 + p // SLOTS + 1))
                need(act, turned, s * NP + p - 1)
                act.activation(mask[:, p % 2], stage[:, p % SLOTS], ACT.Sigmoid, bias=sig_bias[:],
                               scale=1000.0).then_inc(conv_done, 1)

            def copy_oT(s):
                act.wait_ge(c_used, (s + 1) * NK)
                need(act, n_ready, s)
                return act

            def post_a(s, par):
                act.wait_ge(c_used, s * NK + NK)
                act.activation(oT[:], bank[:, par, :], ACT.Copy).then_inc(oT_copied, 1)

            def post_b(s):
                act.wait_ge(mv2_ready, s + 1)
                act.activation(sd2[:], mv2[:, :, 1], ACT.Sqrt, bias=eps[:]).then_inc(sd2_ready, 1)

            def post_c(s):
                act.wait_ge(xt_ready, s + 1)
                act.activation(xnT[:, bass.ds(s * ST, ST)], bank[:, 4, :], ACT.Copy).then_inc(xt_copied, 1)

            def supertile(s, par, first=False, last=False):
                if not first:
                    post_a(s - 1, 1 - par)
                for p in range(NP):
                    if not last:
                        convert(s + 1, p)
                    if p == 3 and not first:
                        post_b(s - 1)
                    if p == 6 and not first:
                        post_c(s - 1)

            for p in range(NP):
                convert(0, p)
            supertile(0, 0, first=True)
            with act.Fori(0, NS // 2 - 1) as i:
                supertile(i * 2 + 1, 1)
                supertile(i * 2 + 2, 0)
            supertile(NS - 1, 1, last=True)
            post_a(NS - 1, 1)
            post_b(NS - 1)
            post_c(NS - 1)

            act.wait_ge(lgd_ready, 1)
            act.activation(pr, lg, ACT.Exp).then_inc(pr_ready, 1)
            for n in range(4):
                act.wait_ge(cwt_ready, n + 1)
                act.activation(cwT[:, 1024 * n:1024 * n + 1024], bank[0:2 * E, n, :].bitcast(F16), ACT.Copy).then_inc(cwt_copied, 1)

            def gelu(j, e):
                for f in range(FC):
                    act.wait_ge(h_ready, FC * j + f + 1)
                    if f == 0:
                        need(act, hw_done, j - 1)
                    act.activation(h[:, e % 2, f], bank[:, 2 * (e % 2) + f, :], ACT.Gelu,
                                   bias=b1T[:, FC * e + f:FC * e + f + 1],
                                   scale=1.0 / (X_SCALE * W_SCALE)).then_inc(gelu_done, 1)

            def high(j, e):
                act.wait_ge(hw_done, j + 1)
                need(act, ffn2_done, j + 1 - HR)
                act.activation(hh[:, e % HR], hw[:, e % 2], ACT.Copy).then_inc(hh_done, 1)

            def copy_y(st):
                act.wait_ge(ffn2_done, (st + 1) * E)
                act.activation(y_sb, bank[:, 6, :], ACT.Copy, scale=1.0 / (C_SCALE * W_SCALE)).then_inc(y_copied, 1)

            def experts(st, first=False):
                for e in range(E):
                    gelu(st * E + e, e)
                    if e or not first:
                        high(st * E + e - 1, (e - 1) % E)
                    if e == LAG and not first:
                        copy_y(st - 1)

            experts(0, first=True)
            with act.Fori(1, NS) as st:
                experts(st)
            high(NS * E - 1, E - 1)
            copy_y(NS - 1)

        @block.vector
        def _(dve):
            steps = [0, 0]

            def link(ins):
                steps[0] += 1
                ins.then_inc(dve_step, 1)
                dve.wait_ge(dve_step, steps[0])

            dve.memset(ones[:], 1.0)
            dve.memset(sig_bias[:], -500.0)
            link(dve.memset(eps[:], LN_EPS))
            dve.drain().then_inc(dve_const, 1)
            dve.wait_ge(small_in, 16 * 11)
            dve.tensor_scalar(b_rep[:], ones[:], b_col[:], None, ALU.mult).then_inc(brep_done, 1)
            dve.wait_ge(xj_in, 64)
            for k in range(NK):
                ins = dve.bn_stats(st1[:, k], x_j[:, k])
            link(ins)
            for k in range(NK):
                ins = dve.bn_aggr(mv1[:, k], st1[:, k])
            ins.then_inc(mv1_ready, 1)
            dve.wait_ge(gc_done, 1)
            link(dve.tensor_copy(G[:], bank[:, 5, 0:2]))
            dve.tensor_tensor(c12[:], bank[:, 5, 2:4], gb12[:], ALU.add)
            link(dve.tensor_scalar(g1_rep[:], ones[:], G[:, 0:1], None, ALU.mult))
            dve.drain().then_inc(g_copied, 1)
            dve.wait_ge(sd1_ready, 1)
            dve.reciprocal(rs1[:], sd1[:]).then_inc(rs1_ready, 1)
            dve.wait_ge(rs1_ready, 1)
            dve.wait_ge(f_ready, 1)
            dve.tensor_copy(f_sb[:], bank[:, 5, 0:2 * NK].rearrange("p (k c) -> p k c", c=2)).then_inc(f_copied, 1)
            dve.wait_ge(f_copied, 1)
            link(dve.tensor_scalar(nf2[:], f_sb[:, :, 1], -1.0, None, ALU.mult))
            dve.tensor_reduce(part_max[:, 0:1], f_sb[:, :, 0], AX_X, ALU.max)
            dve.tensor_reduce(part_max[:, 1:2], f_sb[:, :, 1], AX_X, ALU.max)
            dve.tensor_reduce(part_max[:, 2:3], nf2[:], AX_X, ALU.max).then_inc(pmax_ready, 1)
            dve.wait_ge(amax_ready, 1)
            F1, F2, NF2 = all_max[:, 0:1], all_max[:, 1:2], all_max[:, 2:3]
            tt = lambda o, a, b, op: dve.tensor_tensor(o, a, b, op)
            link(tt(tmp[:, 0:1], c12[:, 0:1], c12[:, 1:2], ALU.add))
            tt(tmp[:, 1:2], tmp[:, 0:1], F2, ALU.add)
            link(tt(tmp[:, 2:3], F2, NF2, ALU.add))
            link(tt(tmp[:, 3:4], tmp[:, 1:2], F1, ALU.add))
            link(tt(tmp[:, 4:5], tmp[:, 3:4], tmp[:, 2:3], ALU.max))
            link(dve.tensor_scalar(tmp[:, 5:6], tmp[:, 4:5], STEEP, None, ALU.mult))
            dve.scalar_tensor_tensor(bias_g[:], tmp[:, 1:2], STEEP, tmp[:, 5:6], ALU.mult, ALU.subtract)
            dve.scalar_tensor_tensor(bias_r[:], F2, STEEP, tmp[:, 5:6], ALU.mult, ALU.subtract)
            dve.tensor_scalar(bias_u[:], F2, -1.0, None, ALU.mult).then_inc(bias_ready, 1)
            dve.wait_ge(ru_exp, 2)
            link(tt(ru[:], rs1[:], u_col[:], ALU.mult))
            for k in range(NK):
                ins = dve.tensor_scalar(Y[:, k], x_j[:, k], mv1[:, k, 0:1], ru[:, k:k + 1], ALU.subtract, ALU.mult)
            link(ins)
            dve.tensor_copy(Y[:, :, D - 1], u_col[:]).then_inc(y_rows, 1)

            at = maskT[:].rearrange("p r s b i e -> p r s b e i")
            at32v = maskT[:].rearrange("p r s b i e -> p r s (b i e)").bitcast(U32)
            mask32 = mask[:].rearrange("p r s j -> p r (s j)").bitcast(U32)

            def turn(s, p, par):
                dve.wait_ge(conv_done, s * NP + p + 1)
                dve.transpose(at32v[:, par, PS_ * p:PS_ * p + PS_, :].rearrange("p s w -> p (s w)"),
                              mask32[:, p % 2]).then_inc(turned, 1)

            POST = 8

            def post_chain(s):
                n = [0]

                def post_link(ins):
                    n[0] += 1
                    ins.then_inc(post_step, 1)
                    dve.wait_ge(post_step, s * POST + n[0])
                return post_link

            sums = bank[:, 2:4, :].rearrange("p b (t c) -> p (b t) c", c=256)

            def post_a(s):
                link_ = post_chain(s)
                dve.wait_ge(n_ready, s + 1)
                link_(dve.tensor_scalar(empty[:], sums[:, :, D], 0.0, None, ALU.is_equal))
                for t in range(TS):
                    ins = dve.scalar_tensor_tensor(fin[:, t], all_rows[:], empty[:, t:t + 1], sums[:, t, 0:D + 1],
                                                   ALU.mult, ALU.add)
                link_(ins)
                link_(dve.reciprocal(rinv[:], fin[:, :, D]))
                for t in range(TS):
                    xt = x2[:, bass.ds(s * TS + t, 1), :].rearrange("p a d -> p (a d)")
                    ins = dve.scalar_tensor_tensor(xs[:, t], fin[:, t, 0:D], rinv[:, t:t + 1], xt, ALU.mult, ALU.add)
                link_(ins)
                for t in range(TS):
                    ins = dve.bn_stats(st2[:, t], xs[:, t])
                dve.tensor_copy(x2[:, bass.ds(s * TS, TS), :], xs[:])
                link_(ins)
                dve.tensor_tensor(diff[:], st2[:, :, 1], st2[:, :, 4], ALU.subtract)
                dve.tensor_tensor(mv2[:, :, 0], st2[:, :, 1], st2[:, :, 4], ALU.add)
                link_(dve.tensor_tensor(mv2[:, :, 1], st2[:, :, 2], st2[:, :, 5], ALU.add))
                dve.tensor_scalar(mv2[:, :, 0], mv2[:, :, 0], 0.5, None, ALU.mult)
                link_(dve.scalar_tensor_tensor(diff[:], diff[:], 0.25, diff[:], ALU.mult, ALU.mult))
                dve.scalar_tensor_tensor(mv2[:, :, 1], mv2[:, :, 1], 1.0 / D, diff[:], ALU.mult,
                                         ALU.add).then_inc(mv2_ready, 1)

            def post_b(s):
                dve.wait_ge(sd2_ready, s + 1)
                dve.reciprocal(rs2[:], sd2[:]).then_inc(post_step, 1)
                dve.wait_ge(post_step, s * POST + POST)
                for t in range(TS):
                    ins = dve.tensor_scalar(xn2[:, t], xs[:, t], mv2[:, t, 0:1], rs2[:, t:t + 1], ALU.subtract, ALU.mult)
                ins.then_inc(xn2_ready, 1)

            def post_c(s):
                cols = bass.ds(s * ST, ST)
                dve.wait_ge(xt_copied, s + 1)
                dve.tensor_scalar(xh[:, cols], xnT[:, cols], X_SCALE, None, ALU.mult).then_inc(xh_ready, 1)
                dve.wait_ge(xh_ready, s + 1)
                dve.scalar_tensor_tensor(xl[:, cols], xnT[:, cols], X_SCALE, xh[:, cols], ALU.mult,
                                         ALU.subtract).then_inc(xl_ready, 1)

            def split_weights():
                dve.wait_ge(w_in, 32)
                for raw, hi, lo in ((w1raw, w1h[:], w1l[:]), (w2raw, w2h[:], w2l[:]), (b2_sb[:], b2h[:], b2l[:])):
                    link(dve.tensor_scalar(hi, raw, W_SCALE, None, ALU.mult))
                    ins = dve.scalar_tensor_tensor(lo, raw, W_SCALE, hi, ALU.mult, ALU.subtract)
                ins.then_inc(wsplit, 1)

            def supertile(s, par, first=False, last=False):
                for k in range(NK):
                    if k == 0:
                        dve.wait_ge(turned, (s + 1) * NP)
                    if first and k == 0:
                        dve.wait_ge(grow_ready, NB)
                    need(dve, c_used, s * NK + k - CR + 1)
                    dve.scalar_tensor_tensor(
                        c[:, k % CR].rearrange("p (s i) -> p s i", i=32),
                        g_row[:, bass.ds(s * ST, ST)].rearrange("p (s i) -> p s i", i=32), r_col[:, k:k + 1],
                        at[:, par, :, k // 4, k % 4, :], ALU.max, ALU.mult).then_inc(c_ready, 1)
                    if k % 4 == 3 and not last:
                        turn(s + 1, k // 4, 1 - par)
                    if not first and k == 12:
                        post_a(s - 1)
                    if not first and k == 20:
                        post_b(s - 1)
                    if not first and k == 29:
                        post_c(s - 1)
                    if first and k == 16:
                        dve.wait_ge(xn_in, 16)
                        split_weights()
                        dve.wait_ge(S_ready, 1)
                        dve.tensor_copy(all_rows[:, 0:D], bank[:, 5, 0:D]).then_inc(dve_step, 1)
                        steps[0] += 1

            for p in range(NP):
                turn(0, p, 0)
            supertile(0, 0, first=True)
            dve.wait_ge(dve_step, steps[0])
            with dve.Fori(0, NS // 2 - 1) as i:
                supertile(i * 2 + 1, 1)
                supertile(i * 2 + 2, 0)
            supertile(NS - 1, 1, last=True)
            post_a(NS - 1)
            post_b(NS - 1)
            post_c(NS - 1)

            tok = lambda v: rowv[:, v, :].unsqueeze(2).to_broadcast([P, NK, E])
            over = lambda t: t.unsqueeze(1).to_broadcast([P, NK, E])
            dve.wait_ge(lg_ready, 1)
            link(tt(lg, bank[:, 5, 0:NK * E].rearrange("p (n e) -> p n e", e=E), over(gateb_sb[:]), ALU.add))
            link(dve.tensor_reduce(rowv[:, 0], lg, AX_X, ALU.max))
            tt(lg, lg, tok(0), ALU.subtract).then_inc(lgd_ready, 1)
            dve.wait_ge(pr_ready, 1)
            dve.tensor_reduce(rowv[:, 1], pr, AX_X, ALU.add)
            link(dve.tensor_reduce(rowv[:, 2], pr, AX_X, ALU.max))
            for chosen in (sel1, sel2):
                link(tt(code, pr if chosen is sel1 else lg, tok(2), ALU.is_equal))
                link(tt(code, code, over(order[:]), ALU.mult))
                link(dve.tensor_reduce(rowv[:, 3], code, AX_X, ALU.max))
                link(tt(chosen, code, tok(3), ALU.is_equal))
                if chosen is sel1:
                    link(dve.scalar_tensor_tensor(lg, sel1, -2.0, pr, ALU.mult, ALU.add))
                    link(dve.tensor_reduce(rowv[:, 2], lg, AX_X, ALU.max))
            link(tt(sel1, sel1, sel2, ALU.add))
            link(dve.reciprocal(rowv[:, 0], rowv[:, 1]))
            link(tt(pr, pr, sel1, ALU.mult))
            link(dve.scalar_tensor_tensor(pr, pr, C_SCALE, tok(0), ALU.mult, ALU.mult))
            link(dve.tensor_copy(cw16[:, :, 0:E], pr))
            tt(cw16[:, :, E:2 * E], pr, cw16[:, :, 0:E], ALU.subtract).then_inc(cw_ready, 1)

            def weigh(j, e):
                dve.wait_ge(gelu_done, FC * (j + 1))
                dve.wait_ge(web_ready, j + 1)
                need(dve, hl_done, j - 1)
                dve.tensor_tensor(hw[:, e % 2], h[:, e % 2], bank[:, 4 + e % 2, :].unsqueeze(1).to_broadcast([P, FC, ST]),
                                  ALU.mult).then_inc(hw_done, 1)

            def low(j, e):
                dve.wait_ge(hh_done, j + 1)
                need(dve, ffn2_done, j + 1 - HR)
                dve.tensor_tensor(hl[:, e % HR], hw[:, e % 2], hh[:, e % HR], ALU.subtract).then_inc(hl_done, 1)

            def add_out(st):
                dve.wait_ge(yt_ready, st + 1)
                dve.wait_ge(out_free, st * 16 + 1)
                dve.tensor_tensor(out_sb, bank[:, 7, :].rearrange("p (t d) -> p t d", d=D),
                                  x2[:, bass.ds(st * TS, TS), :], ALU.add).then_inc(out_added, 1)

            def experts(st, first=False):
                for e in range(E):
                    weigh(st * E + e, e)
                    if e or not first:
                        low(st * E + e - 1, (e - 1) % E)
                    if e == LAG + 1 and not first:
                        add_out(st - 1)

            dve.memset(eps[:], LN_EPS).then_inc(out_free, 1)
            experts(0, first=True)
            with dve.Fori(1, NS) as st:
                experts(st)
            low(NS * E - 1, E - 1)
            add_out(NS - 1)

        @block.tensor
        def _(pe):
            mm = pe.matmul
            pe.wait_ge(brep_done, 1)
            mm(bank[:, 5, 0:2], W_sb[:], w_col[:], start=True, stop=True)
            mm(bank[:, 5, 2:4], b_rep[:], w_col[:], start=True, stop=True).then_inc(gc_done, 1)
            pe.wait_ge(pool_const, 1)
            pe.wait_ge(in2_in, 64)
            for b in range(NB):
                need(pe, in2t_copied, b - 1)
                for e in range(4):
                    ins = pe.transpose(bank[:, 6 + b % 2, P * e:P * e + P], in2_j[:, 4 * b + e], ident[:])
                ins.then_inc(in2t_ready, 1)
            pe.transpose(bank[:, 4, 0:E * FC], b1_sb[:], ident[0:E * FC, 0:E * FC]).then_inc(b1_ready, 1)
            pe.wait_ge(in2t_copied, NB)
            pe.wait_ge(g_copied, 1)
            for k in range(NK):
                ins = mm(bank[:, 5, 2 * k:2 * k + 2], in2T[:, P * k:P * k + P], G[:], start=True, stop=True)
            ins.then_inc(f_ready, 1)
            for b in range(NB):
                need(pe, grow_ready, b - 1)
                mm(bank[:, 6 + b % 2, :], g1_rep[:], in2T[:, 512 * b:512 * b + 512], start=True, stop=True).then_inc(f1row_ready, 1)

            sums = bank[:, 2:4, :].rearrange("p b (t c) -> p (b t) c", c=256)

            def post_a(s):
                pe.wait_ge(oT_copied, s + 1)
                for t in range(TS):
                    ins = mm(sums[:, t, 0:D + 1], oT[:, P * t:P * t + P], back[:, 0:D + 1], start=True, stop=True)
                ins.then_inc(n_ready, 1)

            def post_b(s):
                pe.wait_ge(xn2_ready, s + 1)
                for t in range(TS):
                    ins = pe.transpose(bank[:, 4, P * t:P * t + P], xn2[:, t], ident[:])
                ins.then_inc(xt_ready, 1)

            def supertile(s, par, first=False):
                for k in range(NK):
                    pe.wait_ge(c_ready, s * NK + k + 1)
                    mm(bank[:, par, :], Y[:, k], c[:, k % CR], start=(k == 0), stop=(k == NK - 1)).then_inc(c_used, 1)
                    if first and k == 8:
                        pe.wait_ge(xin_sum, 1)
                        pe.wait_ge(f_copied, 1)
                        mm(bank[:, 5, 0:D], ones[:], xin[:, 0], start=True, stop=True).then_inc(S_ready, 1)
                    if not first and k == 6:
                        post_a(s - 1)
                    if not first and k == 26:
                        post_b(s - 1)

            pe.wait_ge(y_rows, 1)
            pe.wait_ge(b1_copied, 1)
            supertile(0, 0, first=True)
            with pe.Fori(0, NS // 2 - 1) as i:
                supertile(i * 2 + 1, 1)
                supertile(i * 2 + 2, 0)
            supertile(NS - 1, 1)
            post_a(NS - 1)
            post_b(NS - 1)

            pe.wait_ge(xt_copied, NS)
            for n in range(NK):
                ins = mm(bank[:, 5, E * n:E * n + E], xnT[:, P * n:P * n + P], gate_sb[:], start=True, stop=True)
            ins.then_inc(lg_ready, 1)
            pe.wait_ge(cw_ready, 1)
            for n in range(4):
                dst = bank[0:2 * E, n, :].bitcast(F16)
                for t in range(8):
                    ins = pe.transpose(dst[:, P * t:P * t + P], cw16[:, 8 * n + t], ident16[:])
                ins.then_inc(cwt_ready, 1)
            pe.wait_ge(cwt_copied, 4)
            pe.wait_ge(xl_ready, NS)
            pe.wait_ge(wsplit, 1)

            def ffn1(j, e, st):
                cols = bass.ds(st * ST, ST)
                need(pe, hw_done, j - 1)
                need(pe, gelu_done, FC * (j - 1))
                for f in range(FC):
                    wh, wl = w1h[:, e, P * f:P * f + P], w1l[:, e, P * f:P * f + P]
                    dst = bank[:, 2 * (e % 2) + f, :]
                    mm(dst, wh, xh[:, cols], start=True, stop=False)
                    mm(dst, wh, xl[:, cols], start=False, stop=False)
                    mm(dst, wl, xh[:, cols], start=False, stop=True).then_inc(h_ready, 1)
                mm(bank[:, 4 + e % 2, :], sel[:, e], cwT[:, cols], start=True, stop=True).then_inc(web_ready, 1)

            def ffn2(j, e, st):
                dst = bank[:, 6, :]
                if e == 0:
                    need(pe, y_copied, st)
                pe.wait_ge(hl_done, j + 1)
                for f in range(FC):
                    wh, wl, r = w2h[:, FC * e + f], w2l[:, FC * e + f], e % HR
                    mm(dst, wh, hh[:, r, f], start=(e == 0 and f == 0), stop=False)
                    mm(dst, wh, hl[:, r, f], start=False, stop=False)
                    ins = mm(dst, wl, hh[:, r, f], start=False, stop=(e == E - 1 and f == FC - 1))
                ins.then_inc(ffn2_done, 1)
                if e == 0:
                    cols = bass.ds(st * ST, ST)
                    mm(dst, b2h[:], cwT[:, cols], start=False, stop=False)
                    mm(dst, b2l[:], cwT[:, cols], start=False, stop=False)

            def turn_y(st):
                pe.wait_ge(y_copied, st + 1)
                for t in range(TS):
                    ins = pe.transpose(bank[:, 7, P * t:P * t + P], y_sb[:, P * t:P * t + P], ident[:])
                ins.then_inc(yt_ready, 1)

            def experts(st, first=False):
                for e in range(E):
                    ffn1(st * E + e, e, st)
                    if e >= LAG:
                        ffn2(st * E + e - LAG, e - LAG, st)
                    elif not first:
                        ffn2(st * E + e - LAG, e - LAG + E, st - 1)
                    if e == LAG and not first:
                        turn_y(st - 1)

            experts(0, first=True)
            with pe.Fori(1, NS) as st:
                experts(st)
            for e in range(E - LAG, E):
                ffn2((NS - 1) * E + e, e, NS - 1)
            turn_y(NS - 1)


_INS = ["x", "adj", "L0_gnn_inlayer2", "L0_gnn_W", "L0_gnn_b", "L0_gnn_w1", "L0_gnn_b1", "L0_gnn_w2", "L0_gnn_b2",
        "L0_ffn_gate_w", "L0_ffn_gate_b", "L0_ffn_W1", "L0_ffn_b1", "L0_ffn_W2", "L0_ffn_b2"]


def kernel(**inputs):
    import numpy as np
    import concourse.bacc as bacc
    from concourse.bass_utils import run_bass_kernel_spmd

    nc = bacc.Bacc("TRN2", target_bir_lowering=False, num_devices=1)
    arrays, args = {}, []
    for name in _INS:
        a = np.ascontiguousarray(inputs[name])
        arrays[f"in_{name}"] = a
        args.append(nc.dram_tensor(f"in_{name}", a.shape, mybir.dt.from_np(a.dtype), kind="ExternalInput").ap())
    out = nc.dram_tensor("out", inputs["x"].shape, F32, kind="ExternalOutput").ap()
    gnn_moe_kernel(nc, *args, out)
    r = run_bass_kernel_spmd(nc, [arrays], core_ids=[0])
    return r.results[0]["out"]
```

```python
from contextlib import ExitStack

import concourse.bass as bass
from concourse import mybir

P = 128
ALU = mybir.AluOpType
ACT = mybir.ActivationFunctionType
F32 = mybir.dt.float32
F16 = mybir.dt.float16
U8 = mybir.dt.uint8
U32 = mybir.dt.uint32
I32 = mybir.dt.int32
AX_X = mybir.AxisListType.X
RMAX = bass.bass_isa.ReduceOp.max

SLOPE = 0.01
STEEP = 1.0 - SLOPE
LN_EPS = 1e-5

X_SCALE = 1024.0
W_SCALE = 256.0
C_SCALE = 64.0


def gnn_moe_kernel(nc, x, adj, in2, gnn_w, gnn_b, gnn_w1, gnn_b1, gnn_w2, gnn_b2,
                   gate_w, gate_b, W1, b1, W2, b2, shares, out):
    N, D = x.shape
    E, _, H = W1.shape
    NK = N // P
    ST = 512
    NS = N // ST
    TS = ST // P
    Q = 4
    QJ = N // Q
    NB = QJ // P
    PR = 64
    NP = ST // PR
    PS_ = PR // 32
    SLOTS = 4
    CR = 4
    FC = H // P
    LAG = 3
    assert D == P and NS % 2 == 0 and E % 4 == 0 and FC == 2 and NP == 2 * SLOTS

    with ExitStack() as ctx:
        def sb(name, shape, dt=F32):
            return ctx.enter_context(nc.sbuf_tensor(name, shape, dt))

        def sem(name):
            return ctx.enter_context(nc.semaphore(name))

        bank = ctx.enter_context(nc.psum_tensor("bank", [P, 8, 512], F32))

        stage = sb("stage", [P, SLOTS, PS_, QJ], I32)
        maskT = sb("maskT", [P, 2, ST // 32, NB, 32, 4], U8)
        mask = sb("mask", [P, 2, PS_, QJ], U8)
        g_row = sb("g_row", [P, N])
        Y = sb("Y", [P, NK, D])
        x2 = sb("x2", [P, NK, D])
        share1 = sb("share1", [P, N])
        share2 = sb("share2", [P, N])
        share3 = sb("share3", [P, N])
        c = sb("c", [P, CR, ST])
        w1h = sb("w1h", [P, E, H], F16)
        w1l = sb("w1l", [P, E, H], F16)
        w2h = sb("w2h", [P, E * FC, D], F16)
        w2l = sb("w2l", [P, E * FC, D], F16)

        in2_j = share1[:, :].rearrange("p (k d) -> p k d", d=D)
        xin = in2_j
        xh = share2[:, 0:N // 2].bitcast(F16)
        xl = share2[:, N // 2:N].bitcast(F16)
        x_j = share3[:, :].rearrange("p (k d) -> p k d", d=D)
        w1raw = share3[:, 0:E * H].rearrange("p (e f) -> p e f", e=E)
        w2raw = share3[:, E * H:2 * E * H].rearrange("p (c d) -> p c d", d=D)

        ones = sb("ones", [P, P])
        ident = sb("ident", [P, P])
        ident16 = sb("ident16", [P, P], F16)
        back = sb("back", [P, D + 2])
        W_sb = sb("W_sb", [P, D])
        w_col = sb("w_col", [P, 2])
        b_col = sb("b_col", [P, 1])
        gb12 = sb("gb12", [P, 2])
        c12 = sb("c12", [P, 2])
        f1_col = sb("f1_col", [P, NK])
        f2_col = sb("f2_col", [P, NK])
        nf2 = sb("nf2", [P, NK])
        part_max = sb("part_max", [P, 3])
        all_max = sb("all_max", [P, 3])
        tmp = sb("tmp", [P, 8])
        bias_g = sb("bias_g", [P, 1])
        bias_r = sb("bias_r", [P, 1])
        bias_u = sb("bias_u", [P, 1])
        eps = sb("eps", [P, 1])
        nmr = sb("nmr", [P, TS])
        gate_h = sb("gate_h", [P, E], F16)
        gate_l = sb("gate_l", [P, E], F16)
        sig_bias = sb("sig_bias", [P, 1])
        r_col = sb("r_col", [P, NK])
        u_col = sb("u_col", [P, NK])
        ru = sb("ru", [P, NK])
        nmru = sb("nmru", [P, NK])
        st1 = sb("st1", [P, NK, 6])
        mv1 = sb("mv1", [P, NK, 2])
        sd1 = sb("sd1", [P, NK])
        rs1 = sb("rs1", [P, NK])
        all_rows = sb("all_rows", [P, D + 1])
        oT = sb("oT", [P, ST])
        empty = sb("empty", [P, ST], F16)
        all_h = sb("all_h", [P, D + 1], F16)
        all_l = sb("all_l", [P, D + 1], F16)
        rinv = sb("rinv", [P, TS])
        st2 = sb("st2", [P, TS, 6])
        mv2 = sb("mv2", [P, TS, 2])
        sd2 = sb("sd2", [P, TS])
        rs2 = sb("rs2", [P, TS])
        xn2 = sb("xn2", [P, TS, D])
        xs = sb("xs", [P, TS, D])
        xown = sb("xown", [P, TS, D])
        gate_sb = sb("gate_sb", [P, E])
        gateb_sb = sb("gateb_sb", [P, E])
        order = sb("order", [P, E])
        b1_sb = sb("b1_sb", [E * FC, P])
        b1T = sb("b1T", [P, E * FC])
        b2_sb = sb("b2_sb", [2 * E, D])
        b2h = sb("b2h", [2 * E, D], F16)
        b2l = sb("b2l", [2 * E, D], F16)

        stage32 = stage[:].rearrange("p a b c -> p (a b c)").bitcast(F32)
        h = stage32[:, 0:2 * FC * ST].rearrange("p (r f t) -> p r f t", r=2, f=FC)
        hw = stage32[:, 2 * FC * ST:4 * FC * ST].rearrange("p (r f t) -> p r f t", r=2, f=FC)
        at32 = maskT[:].rearrange("p a b c d e -> p (a b c d e)").bitcast(F32)
        HR = 4
        hh = at32[:, 0:HR * FC * ST // 2].bitcast(F16).rearrange("p (r f t) -> p r f t", r=HR, f=FC)
        hl = at32[:, HR * FC * ST // 2:HR * FC * ST].bitcast(F16).rearrange("p (r f t) -> p r f t", r=HR, f=FC)
        gr = share1[:, :]
        lg = gr[:, 0:256].rearrange("p (n e) -> p n e", e=E)
        pr = gr[:, 256:512].rearrange("p (n e) -> p n e", e=E)
        code = gr[:, 512:768].rearrange("p (n e) -> p n e", e=E)
        sel1 = gr[:, 768:1024].rearrange("p (n e) -> p n e", e=E)
        sel2 = gr[:, 1024:1280].rearrange("p (n e) -> p n e", e=E)
        rowv = gr[:, 1280:1280 + 4 * NK].rearrange("p (v n) -> p v n", v=4)
        cwT = gr[0:2 * E, 1664:1664 + N // 2].bitcast(F16)
        cwR = gr[:, 3712:3712 + 3 * P].rearrange("p (b t) -> p b t", b=3)
        wb = share3[:, :].rearrange("p (e t) -> p e t", e=E)
        cw16 = gr[:, 1408:1408 + NK * E].bitcast(F16).rearrange("p (n e) -> p n e", e=2 * E)
        y_sb = c[:, 0, :]
        out_sb = c[:, 1, :].rearrange("p (t d) -> p t d", d=D)

        prod1, prod2 = Y, x2
        w_rep = c[:, 2, 0:2 * P].rearrange("p (v d) -> p v d", v=2)
        b_rep = c[:, 2, 2 * P:3 * P]
        G = c[:, 3, 0:2 * D].rearrange("p (v d) -> p v d", v=2)

        small_in = sem("small_in")
        late_in = sem("late_in")
        in2_in = [sem(f"in2_in{i}") for i in range(2)]
        xj_in = sem("xj_in")
        xn_in = sem("xn_in")
        w_in = sem("w_in")
        adj_in = [sem(f"adj_in{i}") for i in range(SLOTS)]
        pool_const = sem("pool_const")
        pool_step = sem("pool_step")
        dve_const = sem("dve_const")
        brep_done = sem("brep_done")
        gc_done = sem("gc_done")
        gate_split = sem("gate_split")
        b2_split = sem("b2_split")
        g_copied = sem("g_copied")
        f1_made = sem("f1_made")
        f2_made = sem("f2_made")
        prod2_ready = sem("prod2_ready")
        pmax_ready = sem("pmax_ready")
        amax_ready = sem("amax_ready")
        bias_ready = sem("bias_ready")
        f1row_ready = sem("f1row_ready")
        grow_ready = sem("grow_ready")
        ru_exp = sem("ru_exp")
        mv1_ready = sem("mv1_ready")
        sd1_ready = sem("sd1_ready")
        rs1_ready = sem("rs1_ready")
        xin_step = sem("xin_step")
        xin_made = sem("xin_made")
        xin_sum = sem("xin_sum")
        S_ready = sem("S_ready")
        all_ready = sem("all_ready")
        y_rows = sem("y_rows")
        w_step = sem("w_step")
        wsplit = sem("wsplit")
        b1_ready = sem("b1_ready")
        b1_copied = sem("b1_copied")
        dve_step = sem("dve_step")
        conv_done = sem("conv_done")
        turned = sem("turned")
        c_ready = sem("c_ready")
        c_used = sem("c_used")
        oT_copied = sem("oT_copied")
        n_ready = sem("n_ready")
        post_step = sem("post_step")
        empty_ready = sem("empty_ready")
        mv2_ready = sem("mv2_ready")
        sd2_ready = sem("sd2_ready")
        rinv_ready = sem("rinv_ready")
        att_ready = sem("att_ready")
        xs_ready = sem("xs_ready")
        xn2_ready = sem("xn2_ready")
        xt_ready = sem("xt_ready")
        x2_kept = sem("x2_kept")
        nmr_ready = sem("nmr_ready")
        lgp_ready = sem("lgp_ready")
        lg_kept = sem("lg_kept")
        xh_ready = sem("xh_ready")
        xl_ready = sem("xl_ready")
        z_ready = sem("z_ready")
        rz_ready = sem("rz_ready")
        route_step = sem("route_step")
        lgd_ready = sem("lgd_ready")
        pr_ready = sem("pr_ready")
        cw_ready = sem("cw_ready")
        cwt_ready = sem("cwt_ready")
        cwt_copied = sem("cwt_copied")
        h_ready = sem("h_ready")
        gelu_done = sem("gelu_done")
        cwr_ready = sem("cwr_ready")
        cwr_copied = sem("cwr_copied")
        shares_out = sem("shares_out")
        wb_in = [sem(f"wb_in{i}") for i in range(2)]
        hw_done = sem("hw_done")
        hh_done = sem("hh_done")
        hl_done = sem("hl_done")
        ffn2_done = sem("ffn2_done")
        y_copied = sem("y_copied")
        yt_ready = sem("yt_ready")
        out_added = sem("out_added")
        out_free = sem("out_free")

        def need(eng, s, v):
            if not (isinstance(v, int) and v <= 0):
                eng.wait_ge(s, v)

        def by_chunk(t):
            return t.rearrange("(q b a e) d -> q a b e d", q=Q, b=NB, a=32, e=4)

        adj_v = adj.rearrange("(t s i) (q j) -> t q i s j", s=PS_, i=32, q=Q)
        out_v = out.rearrange("(n t p) d -> n p t d", t=TS, p=P)
        dst_k = lambda t, q: t[32 * q:32 * q + 32].rearrange("a (b e) d -> a b (e d)", e=4)

        sums = bank[:, 5:8:2, :].rearrange("p b (t c) -> p b t c", c=256)
        ROWS = (1, 2, 5, 6, 7, 0)
        CONV_POOL, CONV_DVE = (2,), (6,)
        AHEAD = 8
        ROUTE = ((0, NK - 2 * TS, 0), (NK - 2 * TS, NK, 1))
        BA = (3, 6, 0)
        GROUPS = ((0, 16), (16, NK - 2 * TS), (NK - 2 * TS, NK))

        block = ctx.enter_context(nc.Block())

        @block.sync
        def _(sp):
            half = NB // 2
            def load_adj(s, p):
                need(sp, conv_done, s * NP + p - SLOTS + 1)
                for q in range(Q):
                    sp.dma_start(stage[32 * q:32 * q + 32, p % SLOTS], adj_v[s * NP + p, q]).then_inc(adj_in[p % SLOTS], 16)

            for b in (0, half):
                for q in range(Q):
                    sp.dma_start(dst_k(in2_j, q)[:, b:b + half],
                                 by_chunk(in2)[q].rearrange("a b e d -> a b (e d)")[:, b:b + half]).then_inc(in2_in[b // half], 16)
            load_adj(0, 0)
            for q in range(Q):
                sp.dma_start(dst_k(x_j, q), by_chunk(x)[q].rearrange("a b e d -> a b (e d)")).then_inc(xj_in, 16)
            for p in range(1, NP):
                load_adj(0, p)
            for p in range(SLOTS):
                load_adj(1, p)
            sp.wait_ge(f2_made, 2)
            sp.dma_start(x2[:], x.rearrange("(n p) d -> p n d", p=P)).then_inc(xn_in, 16)
            for p in range(SLOTS, NP):
                load_adj(1, p)
            for p in range(SLOTS):
                load_adj(2, p)
            sp.wait_ge(y_rows, NK + 1)
            sp.wait_ge(xin_made, 1)
            sp.dma_start(w1raw, W1.rearrange("e d f -> d e f")).then_inc(w_in, 16)
            sp.dma_start(w2raw, W2.rearrange("e (c f) d -> f (e c) d", c=FC)).then_inc(w_in, 16)
            for p in range(SLOTS, NP):
                load_adj(2, p)
            with sp.Fori(3, NS) as s:
                for p in range(NP):
                    load_adj(s, p)
            def share_out(g):
                n0, n1 = GROUPS[g]
                sp.wait_ge(cwr_copied, g + 1)
                sp.dma_start(shares.rearrange("e (n p) -> n e p", p=P)[n0:n1],
                             cwR[0:(n1 - n0) * E, g]).then_inc(shares_out, 16)

            def share_in(st, half):
                es = slice(half * E // 2, (half + 1) * E // 2)
                src = shares[es, bass.ds(st * ST, ST)].rearrange("(a e) t -> a e t", a=1).to_broadcast([P, E // 2, ST])
                sp.dma_start(wb[:, es], src).then_inc(wb_in[half], 16)

            def store(st):
                sp.wait_ge(out_added, st + 1)
                sp.dma_start(out_v[st], out_sb).then_inc(out_free, 16)

            def next_shares(st, half):
                sp.wait_ge(hw_done, (st - 1) * E + (half + 1) * E // 2)
                share_in(st, half)

            sp.wait_ge(wsplit, 2)
            share_out(0)
            share_out(1)
            sp.wait_ge(shares_out, 32)
            share_in(0, 0)
            share_in(0, 1)
            next_shares(1, 0)
            next_shares(1, 1)
            next_shares(2, 0)
            store(0)
            next_shares(2, 1)
            share_out(2)
            sp.wait_ge(shares_out, 48)
            with sp.Fori(3, NS) as st:
                next_shares(st, 0)
                store(st - 2)
                next_shares(st, 1)
            store(NS - 2)
            store(NS - 1)
            sp.wait_ge(out_free, 16 * NS + 1)

        @block.gpsimd
        def _(pool):
            pool.memset(ident[:], 0.0).then_inc(pool_step, 1)
            pool.memset(all_rows[:, D:D + 1], float(N))
            for e in range(E):
                pool.memset(order[:, e:e + 1], float(E - e))
            pool.wait_ge(pool_step, 1)
            pool.affine_select(out=ident[:], in_=ident[:], compare_op=ALU.not_equal, fill=1.0, base=0,
                               pattern=[[-1, P]], channel_multiplier=1).then_inc(pool_step, 1)
            pool.wait_ge(pool_step, 2)
            pool.tensor_copy(ident16[:], ident[:])
            pool.tensor_copy(back[:, 0:D - 1], ident[:, 0:D - 1])
            pool.tensor_scalar(back[:, D - 1:D], ident[:, D - 1:D], -1.0, None, ALU.add)
            pool.tensor_copy(back[:, D:D + 1], ident[:, D - 1:D]).then_inc(pool_step, 1)
            pool.wait_ge(pool_step, 3)
            pool.drain().then_inc(pool_const, 1)
            pool.wait_ge(g_copied, 1)
            for n in range(2):
                pool.wait_ge(in2_in[n], 64)
                part = slice(n * NK // 2, (n + 1) * NK // 2)
                pool.tensor_tensor(prod2[:, part], in2_j[:, part], G[:, 1:2].to_broadcast([P, NK // 2, D]),
                                   ALU.mult).then_inc(prod2_ready, 1)
            pool.wait_ge(pmax_ready, 1)
            pool.partition_all_reduce(all_max[:], part_max[:], P, RMAX).then_inc(amax_ready, 1)

            for p in CONV_POOL:
                pool.wait_ge(adj_in[p % SLOTS], 64 * (p // SLOTS + 1))
                pool.wait_ge(turned, p - 1)
                pool.wait_ge(conv_done, p)
                pool.tensor_scalar(mask[:, p % 2], stage[:, p % SLOTS], 0.0, None, ALU.is_gt).then_inc(conv_done, 1)

            pool.wait_ge(mv1_ready, 1)
            pool.wait_ge(rs1_ready, 1)
            pool.wait_ge(f1_made, 2)
            pool.wait_ge(prod2_ready, 2)
            wide = lambda t: t.unsqueeze(2).to_broadcast([P, NK, D])
            pool.tensor_tensor(xin, x_j, wide(mv1[:, :, 0]), ALU.subtract).then_inc(xin_made, 1)
            pool.wait_ge(xin_made, 1)
            pool.tensor_tensor(xin, xin, wide(rs1[:]), ALU.mult).then_inc(xin_step, 1)
            pool.wait_ge(xin_step, 1)
            n, steps = NK // 2, 3
            while n:
                pool.tensor_tensor(xin[:, 0:n], xin[:, 0:n], xin[:, n:2 * n], ALU.add).then_inc(pool_step, 1)
                steps += 1
                pool.wait_ge(pool_step, steps)
                n //= 2
            pool.drain().then_inc(xin_sum, 1)

            def split(n, raw, hi, lo):
                pool.wait_ge(w_in, 32)
                pool.tensor_scalar(raw, raw, W_SCALE, None, ALU.mult).then_inc(w_step, 1)
                pool.wait_ge(w_step, 2 * n + 1)
                pool.tensor_copy(hi, raw).then_inc(w_step, 1)
                pool.wait_ge(w_step, 2 * n + 2)
                pool.tensor_tensor(lo, raw, hi, ALU.subtract).then_inc(wsplit, 1)

            def post(s):
                own = x2[:, bass.ds(s * TS, TS), :]
                pool.tensor_copy(xown[:], own)
                pool.drain()
                pool.wait_ge(att_ready, s + 1)
                pool.tensor_tensor(xs[:], xn2[:], xown[:], ALU.add).then_inc(xs_ready, 1)
                pool.tensor_tensor(own, xn2[:], xown[:], ALU.add).then_inc(x2_kept, 1)
                pool.drain()

            pool.wait_ge(xn_in, 16)
            post(0)
            split(0, w1raw, w1h[:], w1l[:])
            post(1)
            split(1, w2raw, w2h[:], w2l[:])
            with pool.Fori(2, NS) as s:
                post(s)

        @block.scalar
        def _(act):
            small = [(W_sb[:], gnn_w), (w_col[:, 0:1], gnn_w1.rearrange("(p a) -> p a", a=1)),
                     (w_col[:, 1:2], gnn_w2.rearrange("(p a) -> p a", a=1)),
                     (b_col[:], gnn_b.rearrange("(p a) -> p a", a=1)),
                     (gb12[:, 0:1], gnn_b1.rearrange("(p a) -> p a", a=1).partition_broadcast(P)),
                     (gb12[:, 1:2], gnn_b2.rearrange("(p a) -> p a", a=1).partition_broadcast(P)),
                     (gate_sb[:], gate_w), (gateb_sb[:], gate_b.rearrange("(a e) -> a e", a=1).partition_broadcast(P)),
                     (b1_sb[:], b1.rearrange("e (c f) -> (e c) f", c=FC)),
                     (b2_sb[0:E], b2), (b2_sb[E:2 * E], b2)]
            for n, (dst, src) in enumerate(small):
                if len(src.shape) == 3:
                    src = src.rearrange("p a e -> p (a e)")
                act.dma_start(dst, src).then_inc(small_in if n < 4 else late_in, 16)

            def convert(s, p):
                act.wait_ge(adj_in[p % SLOTS], 64 * (s * 2 + p // SLOTS + 1))
                need(act, turned, s * NP + p - 1)
                act.activation(mask[:, p % 2], stage[:, p % SLOTS], ACT.Sigmoid, bias=sig_bias[:],
                               scale=1000.0).then_inc(conv_done, 1)

            act.wait_ge(dve_const, 1)
            convert(0, 0)
            convert(0, 1)
            act.wait_ge(bias_ready, 1)
            act.activation(r_col[:], f2_col[:], ACT.Exp, bias=bias_r[:], scale=-STEEP).then_inc(ru_exp, 1)
            act.activation(u_col[:], f2_col[:], ACT.Exp, bias=bias_u[:]).then_inc(ru_exp, 1)
            g_nat = g_row[:, :].rearrange("p (q b a e) -> p b q a e", q=Q, b=NB, a=32, e=4)
            for b in range(NB):
                act.wait_ge(f1row_ready, b + 1)
                act.activation(g_nat[:, b], bank[:, ROWS[b % len(ROWS)], :].rearrange("p (e q a) -> p q a e", e=4, q=Q),
                               ACT.Exp, bias=bias_g[:], scale=STEEP).then_inc(grow_ready, 1)
            for p in (3, 4):
                act.wait_ge(conv_done, p)
                convert(0, p)
            act.wait_ge(mv1_ready, 1)
            act.activation(sd1[:], mv1[:, :, 1], ACT.Sqrt, bias=eps[:]).then_inc(sd1_ready, 1)
            act.wait_ge(b1_ready, 1)
            act.activation(b1T[:], bank[:, 3, 0:E * FC], ACT.Copy).then_inc(b1_copied, 1)

            def post_a(s, par):
                act.wait_ge(c_used, s * NK + NK)
                act.activation(oT[:], bank[:, par, :], ACT.Copy).then_inc(oT_copied, 1)

            def post_b(s):
                act.wait_ge(rinv_ready, s + 1)
                for t in range(TS):
                    ins = act.activation(xn2[:, t], sums[:, t // 2, t % 2, 0:D], ACT.Copy, scale=rinv[:, t:t + 1])
                ins.then_inc(att_ready, 1)

            def post_std(s):
                act.wait_ge(mv2_ready, s + 1)
                act.activation(sd2[:], mv2[:, :, 1], ACT.Sqrt, bias=eps[:]).then_inc(sd2_ready, 1)

            def post_c(s):
                act.wait_ge(x2_kept, s + 1)
                act.wait_ge(nmr_ready, s + 1)
                for t in range(TS):
                    ins = act.activation(xn2[:, t], xs[:, t], ACT.Identity, bias=nmr[:, t:t + 1], scale=rs2[:, t:t + 1])
                ins.then_inc(xn2_ready, 1)

            def post_d(s):
                act.wait_ge(xt_ready, s + 1)
                act.activation(xh[:, bass.ds(s * ST, ST)], bank[:, 5, :], ACT.Copy, scale=X_SCALE).then_inc(xh_ready, 1)

            def route_exp(n0, n1, r):
                act.wait_ge(lgd_ready, r + 1)
                act.activation(pr[:, n0:n1], lg[:, n0:n1], ACT.Exp).then_inc(pr_ready, 1)

            def route_copy(n0, n1, r):
                for g in (2,) if r else (0, 1):
                    rows = (GROUPS[g][1] - GROUPS[g][0]) * E
                    act.wait_ge(cwr_ready, 3 if r else 2)
                    act.activation(cwR[0:rows, g], bank[0:rows, 4, P * g:P * g + P], ACT.Copy).then_inc(cwr_copied, 1)
                for n in range(n0, n1, 8):
                    m = min(8, n1 - n)
                    src = bank[0:2 * E, 7 if r else BA[n // 8], 0:m * P // 2].bitcast(F16)
                    act.wait_ge(cwt_ready, n // 8 + 1)
                    act.activation(cwT[:, P * n:P * (n + m)], src, ACT.Copy).then_inc(cwt_copied, 1)

            def supertile(s, par, first=False, last=False):
                for p in range(NP):
                    if first:
                        for k in range(AHEAD + 4 * p, min(AHEAD + 4 * p + 4, NK)):
                            act.activation(Y[:, k, 0:D - 1], x_j[:, k, 0:D - 1], ACT.Identity, bias=nmru[:, k:k + 1],
                                           scale=ru[:, k:k + 1]).then_inc(y_rows, 1)
                    if not last:
                        convert(s + 1, p)
                    if p == 0 and not first:
                        post_a(s - 1, 1 - par)
                    if last and p == 0:
                        route_exp(*ROUTE[0])
                    if p == 2 and not first:
                        post_b(s - 1)
                    if p == 3 and not first:
                        post_std(s - 1)
                    if p == 4 and not first:
                        post_c(s - 1)
                    if p == 5 and not first:
                        post_d(s - 1)

            for p in range(5, NP):
                if p not in CONV_DVE:
                    act.wait_ge(conv_done, p)
                    convert(0, p)
            act.wait_ge(y_rows, AHEAD + 1)
            supertile(0, 0, first=True)
            with act.Fori(0, NS // 2 - 1) as i:
                supertile(i * 2 + 1, 1)
                supertile(i * 2 + 2, 0)
            supertile(NS - 1, 1, last=True)
            route_copy(*ROUTE[0])
            post_a(NS - 1, 1)

            def gelu(j, e):
                for f in range(FC):
                    act.wait_ge(h_ready, FC * j + f + 1)
                    if f == 0:
                        need(act, hw_done, j - 1)
                    act.activation(h[:, e % 2, f], bank[:, 2 * ((e + 1) % 2) + f, :], ACT.Gelu,
                                   bias=b1T[:, FC * e + f:FC * e + f + 1],
                                   scale=1.0 / (X_SCALE * W_SCALE)).then_inc(gelu_done, 1)

            def high(j, e):
                act.wait_ge(hw_done, j + 1)
                need(act, ffn2_done, j + 1 - HR)
                act.activation(hh[:, e % HR], hw[:, e % 2], ACT.Copy).then_inc(hh_done, 1)

            def copy_y(st):
                act.wait_ge(ffn2_done, (st + 1) * E)
                act.activation(y_sb, bank[:, 6, :], ACT.Copy, scale=1.0 / (C_SCALE * W_SCALE)).then_inc(y_copied, 1)

            def experts(st, first=False, second=False):
                for e in range(E):
                    if e == LAG and not first:
                        copy_y(st - 1)
                    if first and e == 1:
                        post_b(NS - 1)
                    gelu(st * E + e, e)
                    if e or not first:
                        high(st * E + e - 1, (e - 1) % E)
                    if first and e == 3:
                        post_std(NS - 1)
                    if first and e == 4:
                        post_c(NS - 1)
                    if first and e == 5:
                        post_d(NS - 1)
                    if second and e == 1:
                        route_exp(*ROUTE[1])
                    if second and e == 6:
                        route_copy(*ROUTE[1])

            experts(0, first=True)
            experts(1, second=True)
            with act.Fori(2, NS) as st:
                experts(st)
            high(NS * E - 1, E - 1)
            copy_y(NS - 1)

        @block.vector
        def _(dve):
            steps = [0, 0]

            def link(ins):
                steps[0] += 1
                ins.then_inc(dve_step, 1)
                dve.wait_ge(dve_step, steps[0])

            dve.memset(ones[:], 1.0)
            dve.memset(sig_bias[:], -500.0)
            link(dve.memset(eps[:], LN_EPS))
            dve.drain().then_inc(dve_const, 1)
            dve.wait_ge(small_in, 64)
            dve.tensor_scalar(w_rep[:, 0], ones[:], w_col[:, 0:1], None, ALU.mult)
            dve.tensor_scalar(w_rep[:, 1], ones[:], w_col[:, 1:2], None, ALU.mult)
            dve.tensor_scalar(b_rep, ones[:], b_col[:], None, ALU.mult).then_inc(brep_done, 1)
            dve.wait_ge(gc_done, 1)
            dve.tensor_copy(G, bank[:, 4, 0:2 * D].rearrange("p (v d) -> p v d", v=2)).then_inc(g_copied, 1)
            dve.wait_ge(g_copied, 1)
            for n in range(2):
                part = slice(n * NK // 2, (n + 1) * NK // 2)
                dve.wait_ge(in2_in[n], 64)
                link(dve.tensor_tensor(prod1[:, part], in2_j[:, part], G[:, 0:1].to_broadcast([P, NK // 2, D]), ALU.mult))
                dve.tensor_reduce(f1_col[:, part], prod1[:, part], AX_X, ALU.add).then_inc(f1_made, 1)
                dve.wait_ge(prod2_ready, n + 1)
                dve.tensor_reduce(f2_col[:, part], prod2[:, part], AX_X, ALU.add).then_inc(f2_made, 1)
            dve.wait_ge(late_in, 16 * 7)
            dve.tensor_tensor(c12[:], bank[:, 4, 2 * D:2 * D + 2], gb12[:], ALU.add)
            dve.wait_ge(f1_made, 2)
            dve.wait_ge(f2_made, 2)
            link(dve.tensor_scalar(nf2[:], f2_col[:], -1.0, None, ALU.mult))
            dve.tensor_reduce(part_max[:, 0:1], f1_col[:], AX_X, ALU.max)
            dve.tensor_reduce(part_max[:, 1:2], f2_col[:], AX_X, ALU.max)
            dve.tensor_reduce(part_max[:, 2:3], nf2[:], AX_X, ALU.max).then_inc(pmax_ready, 1)
            dve.wait_ge(xj_in, 64)
            for k in range(NK // 8):
                dve.bn_stats(st1[:, k], x_j[:, k])
            dve.wait_ge(amax_ready, 1)
            F1, F2, NF2 = all_max[:, 0:1], all_max[:, 1:2], all_max[:, 2:3]
            tt = lambda o, a, b, op: dve.tensor_tensor(o, a, b, op)
            link(tt(tmp[:, 0:1], c12[:, 0:1], c12[:, 1:2], ALU.add))
            tt(tmp[:, 1:2], tmp[:, 0:1], F2, ALU.add)
            link(tt(tmp[:, 2:3], F2, NF2, ALU.add))
            link(tt(tmp[:, 3:4], tmp[:, 1:2], F1, ALU.add))
            link(tt(tmp[:, 4:5], tmp[:, 3:4], tmp[:, 2:3], ALU.max))
            link(dve.tensor_scalar(tmp[:, 5:6], tmp[:, 4:5], STEEP, None, ALU.mult))
            dve.scalar_tensor_tensor(bias_g[:], tmp[:, 1:2], STEEP, tmp[:, 5:6], ALU.mult, ALU.subtract)
            dve.scalar_tensor_tensor(bias_r[:], F2, STEEP, tmp[:, 5:6], ALU.mult, ALU.subtract)
            dve.tensor_scalar(bias_u[:], F2, -1.0, None, ALU.mult).then_inc(bias_ready, 1)

            at = maskT[:].rearrange("p r s b i e -> p r s b e i")
            at32v = maskT[:].rearrange("p r s b i e -> p r s (b i e)").bitcast(U32)
            mask32 = mask[:].rearrange("p r s j -> p r (s j)").bitcast(U32)

            def turn(s, p, par):
                dve.wait_ge(conv_done, s * NP + p + 1)
                dve.transpose(at32v[:, par, PS_ * p:PS_ * p + PS_, :].rearrange("p s w -> p (s w)"),
                              mask32[:, p % 2]).then_inc(turned, 1)

            def convert(p):
                dve.wait_ge(adj_in[p % SLOTS], 64 * (p // SLOTS + 1))
                dve.wait_ge(turned, p - 1)
                dve.wait_ge(conv_done, p)
                dve.tensor_scalar(mask[:, p % 2], stage[:, p % SLOTS], 0.0, None, ALU.is_gt).then_inc(conv_done, 1)

            turn(0, 0, 0)
            for k in range(NK // 8, NK):
                ins = dve.bn_stats(st1[:, k], x_j[:, k])
                if k == NK // 2:
                    turn(0, 1, 0)
                if k == NK - 8:
                    turn(0, 2, 0)
            link(ins)
            for k in range(NK):
                ins = dve.bn_aggr(mv1[:, k], st1[:, k])
            ins.then_inc(mv1_ready, 1)
            dve.wait_ge(ru_exp, 2)
            dve.tensor_copy(Y[:, :, D - 1], u_col[:]).then_inc(y_rows, 1)
            turn(0, 3, 0)
            turn(0, 4, 0)
            dve.wait_ge(sd1_ready, 1)
            dve.reciprocal(rs1[:], sd1[:]).then_inc(rs1_ready, 1)
            dve.wait_ge(rs1_ready, 1)
            dve.wait_ge(mv1_ready, 1)
            link(dve.tensor_tensor(ru[:], rs1[:], u_col[:], ALU.mult))
            dve.scalar_tensor_tensor(nmru[:], mv1[:, :, 0], -1.0, ru[:], ALU.mult, ALU.mult)

            def row_chunk(k):
                dve.tensor_scalar(Y[:, k, 0:D - 1], x_j[:, k, 0:D - 1], mv1[:, k, 0:1], ru[:, k:k + 1],
                                  ALU.subtract, ALU.mult).then_inc(y_rows, 1)

            for k in range(AHEAD):
                row_chunk(k)
            for p in range(5, NP):
                if p in CONV_DVE:
                    convert(p)
                turn(0, p, 0)

            POST = 2

            def post_0(s):
                dve.wait_ge(oT_copied, s + 1)
                dve.tensor_scalar(empty[:], oT[:], 0.0, None, ALU.is_equal).then_inc(empty_ready, 1)

            def post_a(s):
                dve.wait_ge(n_ready, s + 1)
                dve.reciprocal(rinv[:].rearrange("p (b t) -> p b t", b=2), sums[:, :, :, D]).then_inc(rinv_ready, 1)

            def post_b(s, n):
                if n == 0:
                    dve.wait_ge(xs_ready, s + 1)
                    for t in range(TS):
                        ins = dve.bn_stats(st2[:, t], xs[:, t])
                    ins.then_inc(post_step, 1)
                if n == 1:
                    for t in range(TS):
                        ins = dve.bn_aggr(mv2[:, t], st2[:, t])
                    ins.then_inc(mv2_ready, 1)
                if n == 2:
                    dve.wait_ge(sd2_ready, s + 1)
                    dve.reciprocal(rs2[:], sd2[:]).then_inc(post_step, 1)
                if n == 3:
                    dve.scalar_tensor_tensor(nmr[:], mv2[:, :, 0], -1.0, rs2[:], ALU.mult, ALU.mult).then_inc(nmr_ready, 1)

            def post_c(s):
                cols = bass.ds(s * ST, ST)
                dve.wait_ge(xh_ready, s + 1)
                dve.scalar_tensor_tensor(xl[:, cols], bank[:, 5, :], X_SCALE, xh[:, cols], ALU.mult,
                                         ALU.subtract).then_inc(xl_ready, 1)

            def post_d(s):
                dve.wait_ge(lgp_ready, s + 1)
                dve.scalar_tensor_tensor(lg[:, bass.ds(s * TS, TS), :], bank[:, 7, 0:TS * E].rearrange("p (t e) -> p t e", e=E),
                                         1.0 / (X_SCALE * W_SCALE), gateb_sb[:].unsqueeze(1).to_broadcast([P, TS, E]),
                                         ALU.mult, ALU.add).then_inc(lg_kept, 1)

            def route_a(n0, n1, r):
                dve.wait_ge(lg_kept, NS - 2 * (1 - r))
                L = lg[:, n0:n1, :]
                link(dve.tensor_reduce(rowv[:, 0, n0:n1], L, AX_X, ALU.max))
                tt(L, L, rowv[:, 0, n0:n1].unsqueeze(2).to_broadcast([P, n1 - n0, E]), ALU.subtract).then_inc(lgd_ready, 1)

            def route_b(n0, n1, r):
                L, Pr, code_, s1, s2 = (t[:, n0:n1, :] for t in (lg, pr, code, sel1, sel2))
                row = lambda v: rowv[:, v, n0:n1]
                tok = lambda v: row(v).unsqueeze(2).to_broadcast([P, n1 - n0, E])

                def mark(ins):
                    steps[0] += 1
                    ins.then_inc(dve_step, 1)
                    return steps[0]

                dve.wait_ge(pr_ready, r + 1)
                dve.tensor_reduce(row(1), Pr, AX_X, ALU.add)
                done = mark(dve.tensor_reduce(row(2), Pr, AX_X, ALU.max))
                for chosen, t in ((s1, Pr), (s2, L)):
                    yield
                    dve.wait_ge(dve_step, done)
                    done = mark(tt(code_, t, tok(2), ALU.is_equal))
                    yield
                    dve.wait_ge(dve_step, done)
                    done = mark(tt(code_, code_, order[:].unsqueeze(1).to_broadcast([P, n1 - n0, E]), ALU.mult))
                    yield
                    dve.wait_ge(dve_step, done)
                    done = mark(dve.tensor_reduce(row(3), code_, AX_X, ALU.max))
                    yield
                    dve.wait_ge(dve_step, done)
                    done = mark(tt(chosen, code_, tok(3), ALU.is_equal))
                    if chosen is s1:
                        yield
                        dve.wait_ge(dve_step, done)
                        done = mark(dve.scalar_tensor_tensor(L, s1, -2.0, Pr, ALU.mult, ALU.add))
                        yield
                        dve.wait_ge(dve_step, done)
                        done = mark(dve.tensor_reduce(row(2), L, AX_X, ALU.max))
                yield
                dve.wait_ge(dve_step, done)
                dve.reciprocal(row(0), row(1))
                done = mark(tt(s1, s1, s2, ALU.add))
                yield
                dve.wait_ge(dve_step, done)
                done = mark(tt(Pr, Pr, s1, ALU.mult))
                yield
                dve.wait_ge(dve_step, done)
                done = mark(dve.scalar_tensor_tensor(Pr, Pr, C_SCALE, tok(0), ALU.mult, ALU.mult))
                yield
                dve.wait_ge(dve_step, done)
                done = mark(dve.tensor_copy(cw16[:, n0:n1, 0:E], Pr))
                yield
                dve.wait_ge(dve_step, done)
                tt(cw16[:, n0:n1, E:2 * E], Pr, cw16[:, n0:n1, 0:E], ALU.subtract).then_inc(cw_ready, 1)

            ROUTE_STEPS = 16

            BN = (12, 13, 17, 18)

            def supertile(s, par, first=False, last=False):
                router = route_b(*ROUTE[0])
                for k in range(NK):
                    if k == 0:
                        dve.wait_ge(turned, (s + 1) * NP)
                    if first and k == 0:
                        dve.wait_ge(grow_ready, NB)
                    need(dve, c_used, s * NK + k - CR + 1)
                    if not first and k in (BN[1], BN[3]):
                        dve.wait_ge(post_step, (s - 1) * POST + (1 if k == BN[1] else 2))
                    dve.scalar_tensor_tensor(
                        c[:, k % CR].rearrange("p (s i) -> p s i", i=32),
                        g_row[:, bass.ds(s * ST, ST)].rearrange("p (s i) -> p s i", i=32), r_col[:, k:k + 1],
                        at[:, par, :, k // 4, k % 4, :], ALU.max, ALU.mult).then_inc(c_ready, 1)
                    if k % 4 == 3 and not last:
                        turn(s + 1, k // 4, 1 - par)
                    if not first and k == 5:
                        post_0(s - 1)
                    if not first and k == 8:
                        post_a(s - 1)
                    if not first and k in BN:
                        post_b(s - 1, BN.index(k))
                    if not first and k == 25:
                        post_c(s - 1)
                    if not first and k == 30:
                        post_d(s - 1)
                    if first and k == 16:
                        dve.wait_ge(late_in, 16 * 7)
                        link(dve.tensor_scalar(gate_h[:], gate_sb[:], W_SCALE, None, ALU.mult))
                        dve.scalar_tensor_tensor(gate_l[:], gate_sb[:], W_SCALE, gate_h[:], ALU.mult,
                                                 ALU.subtract).then_inc(gate_split, 1)
                        link(dve.tensor_scalar(b2h[:], b2_sb[:], W_SCALE, None, ALU.mult))
                        dve.scalar_tensor_tensor(b2l[:], b2_sb[:], W_SCALE, b2h[:], ALU.mult,
                                                 ALU.subtract).then_inc(b2_split, 1)
                    if last and k == 3:
                        route_a(*ROUTE[0])
                    if last and 9 <= k < 9 + ROUTE_STEPS:
                        next(router, None)
                    if first and k == NK - 2:
                        dve.wait_ge(S_ready, 1)
                        dve.wait_ge(xn_in, 16)
                        link(dve.tensor_copy(all_rows[:, 0:D], bank[:, 3, 0:D]))
                        link(dve.tensor_scalar(all_rows[:], all_rows[:], ident[:, D - 1:D], None, ALU.mult))
                        link(dve.tensor_copy(all_h[:], all_rows[:]))
                        dve.tensor_tensor(all_l[:], all_rows[:], all_h[:], ALU.subtract).then_inc(all_ready, 1)

            supertile(0, 0, first=True)
            with dve.Fori(0, NS // 2 - 1) as i:
                supertile(i * 2 + 1, 1)
                supertile(i * 2 + 2, 0)
            supertile(NS - 1, 1, last=True)

            def weigh(j, e, st):
                dve.wait_ge(gelu_done, FC * (j + 1))
                if e % (E // 2) == 0:
                    dve.wait_ge(wb_in[e // (E // 2)], 16 * (st + 1))
                need(dve, hl_done, j - 1)
                dve.tensor_tensor(hw[:, e % 2], h[:, e % 2], wb[:, e].unsqueeze(1).to_broadcast([P, FC, ST]),
                                  ALU.mult).then_inc(hw_done, 1)

            def low(j, e):
                dve.wait_ge(hh_done, j + 1)
                need(dve, ffn2_done, j + 1 - HR)
                dve.tensor_tensor(hl[:, e % HR], hw[:, e % 2], hh[:, e % HR], ALU.subtract).then_inc(hl_done, 1)

            def add_out(st):
                dve.wait_ge(yt_ready, st + 1)
                dve.wait_ge(out_free, st * 16 + 1)
                dve.tensor_tensor(out_sb, bank[:, 5, :].rearrange("p (t d) -> p t d", d=D),
                                  x2[:, bass.ds(st * TS, TS), :], ALU.add).then_inc(out_added, 1)

            def experts(st, first=False, second=False):
                router = route_b(*ROUTE[1])
                for e in range(E):
                    if first and e == 0:
                        post_0(NS - 1)
                        post_a(NS - 1)
                    weigh(st * E + e, e, st)
                    if e or not first:
                        low(st * E + e - 1, (e - 1) % E)
                    if e == LAG + 1 and not first:
                        add_out(st - 1)
                    if first and e in (2, 3):
                        for n in (0, 1) if e == 2 else (2, 3):
                            if n in (1, 3):
                                dve.wait_ge(post_step, (NS - 1) * POST + (n + 1) // 2)
                            post_b(NS - 1, n)
                    if first and e == 5:
                        post_c(NS - 1)
                    if first and e == 7:
                        post_d(NS - 1)
                    if second and e == 0:
                        route_a(*ROUTE[1])
                    if second and 1 <= e < 5:
                        for _ in range(ROUTE_STEPS // 4):
                            next(router, None)

            dve.memset(eps[:], LN_EPS).then_inc(out_free, 1)
            experts(0, first=True)
            experts(1, second=True)
            with dve.Fori(2, NS) as st:
                experts(st)
            low(NS * E - 1, E - 1)
            add_out(NS - 1)

        @block.tensor
        def _(pe):
            mm = pe.matmul
            pe.wait_ge(brep_done, 1)
            for v in range(2):
                mm(bank[:, 4, D * v:D * v + D], w_rep[:, v], W_sb[:], start=True, stop=True)
            mm(bank[:, 4, 2 * D:2 * D + 2], b_rep, w_col[:], start=True, stop=True).then_inc(gc_done, 1)
            pe.wait_ge(pool_const, 1)
            pe.wait_ge(late_in, 16 * 7)
            pe.transpose(bank[:, 3, 0:E * FC], b1_sb[:], ident[0:E * FC, 0:E * FC]).then_inc(b1_ready, 1)
            for b in range(NB):
                pe.wait_ge(f1_made, 1 if b < NB // 2 else 2)
                need(pe, grow_ready, b - len(ROWS) + 1)
                for e in range(4):
                    k = 4 * b + e
                    ins = mm(bank[:, ROWS[b % len(ROWS)], P * e:P * e + P], f1_col[:, k:k + 1].to_broadcast([P, P]),
                             ident[:], start=True, stop=True)
                ins.then_inc(f1row_ready, 1)

            def post_a(s):
                pe.wait_ge(oT_copied, s + 1)
                for t in range(TS):
                    mm(sums[:, t // 2, t % 2, 0:D + 1], oT[:, P * t:P * t + P], back[:, 0:D + 1], start=True, stop=False)
                    if t == 0:
                        pe.wait_ge(empty_ready, s + 1)
                    mm(sums[:, t // 2, t % 2, 0:D + 1], empty[:, P * t:P * t + P], all_h[:], start=False, stop=False)
                    ins = mm(sums[:, t // 2, t % 2, 0:D + 1], empty[:, P * t:P * t + P], all_l[:], start=False, stop=True)
                ins.then_inc(n_ready, 1)

            def post_b(s):
                pe.wait_ge(xn2_ready, s + 1)
                for t in range(TS):
                    ins = pe.transpose(bank[:, 5, P * t:P * t + P], xn2[:, t], ident[:])
                ins.then_inc(xt_ready, 1)

            def post_c(s):
                pe.wait_ge(xl_ready, s + 1)
                for t in range(TS):
                    toks = bass.ds(s * ST + P * t, P)
                    dst = bank[:, 7, E * t:E * t + E]
                    mm(dst, xh[:, toks], gate_h[:], start=True, stop=False)
                    mm(dst, xl[:, toks], gate_h[:], start=False, stop=False)
                    ins = mm(dst, xh[:, toks], gate_l[:], start=False, stop=True)
                ins.then_inc(lgp_ready, 1)

            def route(n0, n1, r):
                pe.wait_ge(cw_ready, r + 1)
                for g in (2,) if r else (0, 1):
                    a, b = GROUPS[g]
                    pe.transpose(bank[0:(b - a) * E, 4, P * g:P * g + P],
                                 pr[:, a:b, :].rearrange("p n e -> p (n e)"), ident[:]).then_inc(cwr_ready, 1)
                for n in range(n0, n1, 8):
                    m = min(8, n1 - n)
                    dst = bank[0:2 * E, 7 if r else BA[n // 8], :].bitcast(F16)
                    for t in range(m):
                        ins = pe.transpose(dst[:, P * t:P * t + P], cw16[:, n + t], ident16[:])
                    ins.then_inc(cwt_ready, 1)

            def supertile(s, par, first=False, last=False):
                for k in range(NK):
                    if first:
                        pe.wait_ge(y_rows, k + 2)
                    pe.wait_ge(c_ready, s * NK + k + 1)
                    mm(bank[:, par, :], Y[:, k], c[:, k % CR], start=(k == 0), stop=(k == NK - 1)).then_inc(c_used, 1)
                    if first and k == NK - 8:
                        pe.wait_ge(xin_sum, 1)
                        pe.wait_ge(gate_split, 1)
                        mm(bank[:, 3, 0:D], ones[:], xin[:, 0], start=True, stop=True).then_inc(S_ready, 1)
                    if not first and k == 4:
                        post_a(s - 1)
                    if not first and k == 19:
                        post_b(s - 1)
                    if not first and k == 24:
                        post_c(s - 1)
                    if last and k == 25:
                        route(*ROUTE[0])

            pe.wait_ge(b1_copied, 1)
            pe.wait_ge(grow_ready, NB)
            supertile(0, 0, first=True)
            pe.wait_ge(all_ready, 1)
            with pe.Fori(0, NS // 2 - 1) as i:
                supertile(i * 2 + 1, 1)
                supertile(i * 2 + 2, 0)
            supertile(NS - 1, 1, last=True)
            pe.wait_ge(wsplit, 2)
            pe.wait_ge(b2_split, 1)

            def ffn1(j, e, st):
                cols = bass.ds(st * ST, ST)
                need(pe, gelu_done, FC * (j - 1))
                for f in range(FC):
                    wh, wl = w1h[:, e, P * f:P * f + P], w1l[:, e, P * f:P * f + P]
                    dst = bank[:, 2 * ((e + 1) % 2) + f, :]
                    mm(dst, wh, xh[:, cols], start=True, stop=False)
                    mm(dst, wh, xl[:, cols], start=False, stop=False)
                    mm(dst, wl, xh[:, cols], start=False, stop=True).then_inc(h_ready, 1)

            def ffn2(j, e, st):
                dst = bank[:, 6, :]
                if e == 0:
                    need(pe, y_copied, st)
                pe.wait_ge(hl_done, j + 1)
                for f in range(FC):
                    wh, wl, r = w2h[:, FC * e + f], w2l[:, FC * e + f], e % HR
                    mm(dst, wh, hh[:, r, f], start=(e == 0 and f == 0), stop=False)
                    mm(dst, wh, hl[:, r, f], start=False, stop=False)
                    ins = mm(dst, wl, hh[:, r, f], start=False, stop=(e == E - 1 and f == FC - 1))
                ins.then_inc(ffn2_done, 1)
                if e == 0:
                    cols = bass.ds(st * ST, ST)
                    mm(dst, b2h[:], cwT[:, cols], start=False, stop=False)
                    mm(dst, b2l[:], cwT[:, cols], start=False, stop=False)

            def turn_y(st):
                pe.wait_ge(y_copied, st + 1)
                for t in range(TS):
                    ins = pe.transpose(bank[:, 5, P * t:P * t + P], y_sb[:, P * t:P * t + P], ident[:])
                ins.then_inc(yt_ready, 1)

            def experts(st, first=False, second=False):
                for e in range(E):
                    if first and e == 0:
                        pe.wait_ge(cwt_copied, len(BA))
                    if first and e == 1:
                        post_a(NS - 1)
                    ffn1(st * E + e, e, st)
                    if e >= LAG:
                        ffn2(st * E + e - LAG, e - LAG, st)
                    elif not first:
                        ffn2(st * E + e - LAG, e - LAG + E, st - 1)
                    if e == LAG and not first:
                        turn_y(st - 1)
                    if first and e == 5:
                        post_b(NS - 1)
                    if first and e == 6:
                        post_c(NS - 1)
                    if second and e == 5:
                        route(*ROUTE[1])

            experts(0, first=True)
            experts(1, second=True)
            with pe.Fori(2, NS) as st:
                experts(st)
            for e in range(E - LAG, E):
                ffn2((NS - 1) * E + e, e, NS - 1)
            turn_y(NS - 1)


_INS = ["x", "adj", "L0_gnn_inlayer2", "L0_gnn_W", "L0_gnn_b", "L0_gnn_w1", "L0_gnn_b1", "L0_gnn_w2", "L0_gnn_b2",
        "L0_ffn_gate_w", "L0_ffn_gate_b", "L0_ffn_W1", "L0_ffn_b1", "L0_ffn_W2", "L0_ffn_b2"]


def kernel(**inputs):
    import numpy as np
    import concourse.bacc as bacc
    from concourse.bass_utils import run_bass_kernel_spmd

    nc = bacc.Bacc("TRN2", target_bir_lowering=False, num_devices=1)
    arrays, args = {}, []
    for name in _INS:
        a = np.ascontiguousarray(inputs[name])
        arrays[f"in_{name}"] = a
        args.append(nc.dram_tensor(f"in_{name}", a.shape, mybir.dt.from_np(a.dtype), kind="ExternalInput").ap())
    shares = nc.dram_tensor("shares", (inputs["L0_ffn_W1"].shape[0], inputs["x"].shape[0]), F32, kind="Internal").ap()
    out = nc.dram_tensor("out", inputs["x"].shape, F32, kind="ExternalOutput").ap()
    gnn_moe_kernel(nc, *args, shares, out)
    r = run_bass_kernel_spmd(nc, [arrays], core_ids=[0])
    return r.results[0]["out"]
```

```python
from contextlib import ExitStack

import concourse.bass as bass
from concourse import mybir

P = 128
ALU = mybir.AluOpType
ACT = mybir.ActivationFunctionType
F32 = mybir.dt.float32
F16 = mybir.dt.float16
U8 = mybir.dt.uint8
U32 = mybir.dt.uint32
I32 = mybir.dt.int32
AX_X = mybir.AxisListType.X
RMAX = bass.bass_isa.ReduceOp.max

SLOPE = 0.01
STEEP = 1.0 - SLOPE
LN_EPS = 1e-5

X_SCALE = 1024.0
W_SCALE = 256.0
C_SCALE = 64.0


def gnn_moe_kernel(nc, x, adj, in2, gnn_w, gnn_b, gnn_w1, gnn_b1, gnn_w2, gnn_b2,
                   gate_w, gate_b, W1, b1, W2, b2, shares, out):
    N, D = x.shape
    E, _, H = W1.shape
    NK = N // P
    ST = 512
    NS = N // ST
    TS = ST // P
    Q = 4
    QJ = N // Q
    NB = QJ // P
    PR = 64
    NP = ST // PR
    PS_ = PR // 32
    SLOTS = 4
    CR = 4
    PEELED = 3
    FC = H // P
    WARM = 8
    LAG = 3
    assert D == P and NS % 2 == 0 and E % 4 == 0 and FC == 2 and NP == 2 * SLOTS

    with ExitStack() as ctx:
        def sb(name, shape, dt=F32):
            return ctx.enter_context(nc.sbuf_tensor(name, shape, dt))

        def sem(name):
            return ctx.enter_context(nc.semaphore(name))

        bank = ctx.enter_context(nc.psum_tensor("bank", [P, 8, 512], F32))

        stage = sb("stage", [P, SLOTS, PS_, QJ], I32)
        maskT = sb("maskT", [P, 2, ST // 32, NB, 32, 4], U8)
        mask = sb("mask", [P, 2, PS_, QJ], U8)
        g_row = sb("g_row", [P, N])
        Y = sb("Y", [P, NK, D])
        x2 = sb("x2", [P, NK, D])
        share1 = sb("share1", [P, N])
        share2 = sb("share2", [P, N])
        share3 = sb("share3", [P, N])
        c = sb("c", [P, CR, ST])
        w1h = sb("w1h", [P, E, H], F16)
        w1l = sb("w1l", [P, E, H], F16)
        w2h = sb("w2h", [P, E * FC, D], F16)
        w2l = sb("w2l", [P, E * FC, D], F16)

        in2_j = share1[:, :].rearrange("p (k d) -> p k d", d=D)
        xin = in2_j
        xh = share2[:, 0:N // 2].bitcast(F16)
        xl = share2[:, N // 2:N].bitcast(F16)
        x_j = share3[:, :].rearrange("p (k d) -> p k d", d=D)
        w1raw = share3[:, 0:E * H].rearrange("p (e f) -> p e f", e=E)
        w2raw = share3[:, E * H:2 * E * H].rearrange("p (c d) -> p c d", d=D)

        ones = sb("ones", [P, P])
        ident = sb("ident", [P, P])
        ident16 = sb("ident16", [P, P], F16)
        back = sb("back", [P, D + 2])
        W_sb = sb("W_sb", [P, D])
        w_col = sb("w_col", [P, 2])
        b_col = sb("b_col", [P, 1])
        gb12 = sb("gb12", [P, 2])
        c12 = sb("c12", [P, 2])
        f1_col = sb("f1_col", [P, NK])
        f2_col = sb("f2_col", [P, NK])
        nf2 = sb("nf2", [P, NK])
        part_max = sb("part_max", [P, 3])
        all_max = sb("all_max", [P, 3])
        tmp = sb("tmp", [P, 8])
        bias_g = sb("bias_g", [P, 1])
        bias_r = sb("bias_r", [P, 1])
        bias_u = sb("bias_u", [P, 1])
        eps = sb("eps", [P, 1])
        nmr = sb("nmr", [P, TS])
        gate_hl = sb("gate_hl", [P, 2 * E], F16)
        lgl = sb("lgl", [P, TS, E])
        sig_bias = sb("sig_bias", [P, 1])
        r_col = sb("r_col", [P, NK])
        u_col = sb("u_col", [P, NK])
        ru = sb("ru", [P, NK])
        nmru = sb("nmru", [P, NK])
        st1 = sb("st1", [P, NK, 6])
        mv1 = sb("mv1", [P, NK, 2])
        sd1 = sb("sd1", [P, NK])
        rs1 = sb("rs1", [P, NK])
        all_rows = sb("all_rows", [P, D + 1])
        oT = sb("oT", [P, ST])
        empty = sb("empty", [P, ST], F16)
        all_h = sb("all_h", [P, D + 1], F16)
        all_l = sb("all_l", [P, D + 1], F16)
        rinv = sb("rinv", [P, TS])
        st2 = sb("st2", [P, TS, 6])
        mv2 = sb("mv2", [P, TS, 2])
        sd2 = sb("sd2", [P, TS])
        warm = sb("warm", [P, 1])
        rs2 = sb("rs2", [P, TS])
        xn2 = sb("xn2", [P, TS, D])
        xs = sb("xs", [P, TS, D])
        xown = sb("xown", [P, TS, D])
        gate_sb = sb("gate_sb", [P, E])
        gateb_sb = sb("gateb_sb", [P, E])
        order = sb("order", [P, E])
        b1_sb = sb("b1_sb", [E * FC, P])
        b1T = sb("b1T", [P, E * FC])
        b2_sb = sb("b2_sb", [4 * E, D])
        b2h = sb("b2h", [4 * E, D], F16)
        b2l = sb("b2l", [4 * E, D], F16)
        b2hl = sb("b2hl", [4 * E, D], F16)
        upper = sb("upper", [4 * E, 1])
        lower = sb("lower", [4 * E, 1])

        stage32 = stage[:].rearrange("p a b c -> p (a b c)").bitcast(F32)
        h = stage32[:, 0:2 * FC * ST].rearrange("p (r f t) -> p r f t", r=2, f=FC)
        hw = stage32[:, 2 * FC * ST:4 * FC * ST].rearrange("p (r f t) -> p r f t", r=2, f=FC)
        at32 = maskT[:].rearrange("p a b c d e -> p (a b c d e)").bitcast(F32)
        HR = 8
        hh = at32[:, 0:HR * FC * ST // 2].bitcast(F16).rearrange("p (r f t) -> p r f t", r=HR, f=FC)
        hl = at32[:, HR * FC * ST // 2:HR * FC * ST].bitcast(F16).rearrange("p (r f t) -> p r f t", r=HR, f=FC)
        gr = share1[:, :]
        lg = gr[:, 0:256].rearrange("p (n e) -> p n e", e=E)
        pr = gr[:, 256:512].rearrange("p (n e) -> p n e", e=E)
        code = gr[:, 512:768].rearrange("p (n e) -> p n e", e=E)
        sel1 = gr[:, 768:1024].rearrange("p (n e) -> p n e", e=E)
        sel2 = gr[:, 1024:1280].rearrange("p (n e) -> p n e", e=E)
        rowv = gr[:, 1280:1280 + 4 * NK].rearrange("p (v n) -> p v n", v=4)
        cwT = gr[0:4 * E, 1920:1920 + N // 2].bitcast(F16)
        cwR = stage32[:, 4 * FC * ST:4 * FC * ST + 3 * P].rearrange("p (b t) -> p b t", b=3)
        wb = share3[:, :].rearrange("p (e t) -> p e t", e=E)
        cw16 = gr[:, 1408:1408 + 2 * NK * E].bitcast(F16).rearrange("p (n r v e) -> p n r v e", r=2, v=2, e=E)
        y_sb = c[:, 0, :]
        out_sb = c[:, 1, :].rearrange("p (t d) -> p t d", d=D)

        prod1, prod2 = Y, x2
        w_rep = c[:, 2, 0:2 * P].rearrange("p (v d) -> p v d", v=2)
        b_rep = c[:, 2, 2 * P:3 * P]
        G = c[:, 3, 0:2 * D].rearrange("p (v d) -> p v d", v=2)

        small_in = sem("small_in")
        late_in = sem("late_in")
        in2_in = [sem(f"in2_in{i}") for i in range(2)]
        xj_in = sem("xj_in")
        xn_in = [sem(f"xn_in{i}") for i in range(2)]
        w_in = sem("w_in")
        adj_in = [sem(f"adj_in{i}") for i in range(SLOTS)]
        pool_const = sem("pool_const")
        pool_step = sem("pool_step")
        dve_const = sem("dve_const")
        brep_done = sem("brep_done")
        gc_done = sem("gc_done")
        S_step = sem("S_step")
        b2_split = sem("b2_split")
        g_copied = sem("g_copied")
        f1_made = sem("f1_made")
        f2_made = sem("f2_made")
        prod2_ready = sem("prod2_ready")
        pmax_ready = sem("pmax_ready")
        amax_ready = sem("amax_ready")
        bias_ready = sem("bias_ready")
        f1row_ready = sem("f1row_ready")
        grow_ready = sem("grow_ready")
        ru_exp = sem("ru_exp")
        mv1_ready = sem("mv1_ready")
        sd1_ready = sem("sd1_ready")
        rs1_ready = sem("rs1_ready")
        xin_step = sem("xin_step")
        xin_made = sem("xin_made")
        xin_sum = sem("xin_sum")
        S_ready = sem("S_ready")
        all_ready = sem("all_ready")
        y_rows = sem("y_rows")
        w_step = sem("w_step")
        wsplit = sem("wsplit")
        b1_ready = sem("b1_ready")
        b1_copied = sem("b1_copied")
        dve_step = sem("dve_step")
        conv_done = sem("conv_done")
        turned = sem("turned")
        c_ready = sem("c_ready")
        c_used = sem("c_used")
        oT_copied = sem("oT_copied")
        n_ready = sem("n_ready")
        post_step = sem("post_step")
        empty_ready = sem("empty_ready")
        mv2_ready = sem("mv2_ready")
        sd2_ready = sem("sd2_ready")
        rinv_ready = sem("rinv_ready")
        att_ready = sem("att_ready")
        xs_ready = sem("xs_ready")
        xn2_ready = sem("xn2_ready")
        xt_ready = sem("xt_ready")
        x2_kept = sem("x2_kept")
        nmr_ready = sem("nmr_ready")
        lgp_ready = sem("lgp_ready")
        lg_kept = sem("lg_kept")
        xh_ready = sem("xh_ready")
        xl_ready = sem("xl_ready")
        lgd_ready = sem("lgd_ready")
        pr_ready = sem("pr_ready")
        cw_ready = sem("cw_ready")
        cwt_ready = sem("cwt_ready")
        cwt_copied = sem("cwt_copied")
        h_ready = sem("h_ready")
        gelu_done = sem("gelu_done")
        cwr_ready = sem("cwr_ready")
        cwr_copied = sem("cwr_copied")
        shares_out = sem("shares_out")
        wb_in = [sem(f"wb_in{i}") for i in range(2)]
        hw_done = sem("hw_done")
        hh_done = sem("hh_done")
        hl_done = sem("hl_done")
        ffn2_done = sem("ffn2_done")
        y_copied = sem("y_copied")
        yt_ready = sem("yt_ready")
        out_added = sem("out_added")
        out_free = sem("out_free")

        def need(eng, s, v):
            if not (isinstance(v, int) and v <= 0):
                eng.wait_ge(s, v)

        def by_chunk(t):
            return t.rearrange("(q b a e) d -> q a b e d", q=Q, b=NB, a=32, e=4)

        adj_v = adj.rearrange("(t s i) (q j) -> t q i s j", s=PS_, i=32, q=Q)
        out_v = out.rearrange("(n t p) d -> n p t d", t=TS, p=P)
        dst_k = lambda t, q: t[32 * q:32 * q + 32].rearrange("a (b e) d -> a b (e d)", e=4)

        sums = bank[:, 5:8:2, :].rearrange("p b (t c) -> p b t c", c=256)
        ROWS = (1, 2, 5, 6, 7, 0)
        CONV_POOL, CONV_DVE = (0,), (1, 2, 3, 6)
        AHEAD = 8
        ROUTE = ((0, NK - 2 * TS, 0), (NK - 2 * TS, NK, 1))
        BA = (3, 6, 0)
        GROUPS = ((0, 16), (16, NK - 2 * TS), (NK - 2 * TS, NK))

        block = ctx.enter_context(nc.Block())

        @block.sync
        def _(sp):
            half = NB // 2
            def load_adj(s, p):
                need(sp, conv_done, s * NP + p - SLOTS + 1)
                for q in range(Q):
                    sp.dma_start(stage[32 * q:32 * q + 32, p % SLOTS], adj_v[s * NP + p, q]).then_inc(adj_in[p % SLOTS], 16)

            for b in (0, half):
                for q in range(Q):
                    sp.dma_start(dst_k(in2_j, q)[:, b:b + half],
                                 by_chunk(in2)[q].rearrange("a b e d -> a b (e d)")[:, b:b + half]).then_inc(in2_in[b // half], 16)
            load_adj(0, 0)
            for q in range(Q):
                sp.dma_start(dst_k(x_j, q), by_chunk(x)[q].rearrange("a b e d -> a b (e d)")).then_inc(xj_in, 16)
            for p in range(1, NP):
                load_adj(0, p)
            x_rows = x.rearrange("(n p) d -> p n d", p=P)

            def load_half(s, half):
                for p in range(half * SLOTS, (half + 1) * SLOTS):
                    load_adj(s, p)

            load_half(1, 0)
            sp.wait_ge(f2_made, 2)
            sp.dma_start(x2[:, 0:TS], x_rows[:, 0:TS]).then_inc(xn_in[0], 16)
            load_half(1, 1)
            load_half(2, 0)
            sp.dma_start(x2[:, TS:NK], x_rows[:, TS:NK]).then_inc(xn_in[1], 16)
            load_half(2, 1)
            load_half(3, 0)
            sp.wait_ge(y_rows, NK + 1)
            sp.wait_ge(xin_made, 1)
            sp.dma_start(w1raw, W1.rearrange("e d f -> d e f")).then_inc(w_in, 16)
            sp.dma_start(w2raw, W2.rearrange("e (c f) d -> f (e c) d", c=FC)).then_inc(w_in, 16)
            load_half(3, 1)
            with sp.Fori(4, NS) as s:
                load_half(s, 0)
                load_half(s, 1)

            def share_out(g):
                n0, n1 = GROUPS[g]
                sp.wait_ge(cwr_copied, g + 1)
                sp.dma_start(shares.rearrange("e (n p) -> n e p", p=P)[n0:n1],
                             cwR[0:(n1 - n0) * E, g]).then_inc(shares_out, 16)

            def share_in(st, half):
                es = slice(half * E // 2, (half + 1) * E // 2)
                src = shares[es, bass.ds(st * ST, ST)].rearrange("(a e) t -> a e t", a=1).to_broadcast([P, E // 2, ST])
                sp.dma_start(wb[:, es], src).then_inc(wb_in[half], 16)

            def store(st):
                sp.wait_ge(out_added, st + 1)
                sp.dma_start(out_v[st], out_sb).then_inc(out_free, 16)

            def next_shares(st, half):
                sp.wait_ge(hw_done, (st - 1) * E + (half + 1) * E // 2)
                share_in(st, half)

            sp.wait_ge(wsplit, 4)
            share_out(0)
            share_out(1)
            sp.wait_ge(shares_out, 32)
            share_in(0, 0)
            share_in(0, 1)
            next_shares(1, 0)
            next_shares(1, 1)
            next_shares(2, 0)
            store(0)
            next_shares(2, 1)
            next_shares(3, 0)
            store(1)
            next_shares(3, 1)
            share_out(2)
            sp.wait_ge(shares_out, 48)
            with sp.Fori(4, NS) as st:
                next_shares(st, 0)
                store(st - 2)
                next_shares(st, 1)
            store(NS - 2)
            store(NS - 1)
            sp.wait_ge(out_free, 16 * NS + 1)

        @block.gpsimd
        def _(pool):
            pool.memset(lower[:], 1.0).then_inc(pool_step, 1)
            pool.memset(ident[:], 0.0).then_inc(pool_step, 1)
            pool.memset(all_rows[:, D:D + 1], float(N))
            for e in range(E):
                pool.memset(order[:, e:e + 1], float(E - e))
            pool.wait_ge(pool_step, 2)
            pool.affine_select(out=ident[:], in_=ident[:], compare_op=ALU.not_equal, fill=1.0, base=0,
                               pattern=[[-1, P]], channel_multiplier=1).then_inc(pool_step, 1)
            pool.wait_ge(pool_step, 3)
            pool.tensor_copy(ident16[:], ident[:])
            pool.tensor_copy(back[:, 0:D - 1], ident[:, 0:D - 1])
            pool.tensor_scalar(back[:, D - 1:D], ident[:, D - 1:D], -1.0, None, ALU.add)
            pool.tensor_copy(back[:, D:D + 1], ident[:, D - 1:D]).then_inc(pool_step, 1)
            pool.wait_ge(pool_step, 4)
            pool.drain().then_inc(pool_const, 1)
            pool.affine_select(out=lower[:], in_=lower[:], compare_op=ALU.is_ge, fill=0.0, base=-2 * E,
                               pattern=[[0, 1]], channel_multiplier=1).then_inc(pool_step, 1)
            pool.wait_ge(pool_step, 5)
            pool.tensor_scalar(upper[:], lower[:], -1.0, 1.0, ALU.mult, ALU.add).then_inc(pool_step, 1)
            pool.wait_ge(g_copied, 1)
            for n in range(2):
                pool.wait_ge(in2_in[n], 64)
                part = slice(n * NK // 2, (n + 1) * NK // 2)
                pool.tensor_tensor(prod2[:, part], in2_j[:, part], G[:, 1:2].to_broadcast([P, NK // 2, D]),
                                   ALU.mult).then_inc(prod2_ready, 1)
            for p in CONV_POOL:
                pool.wait_ge(adj_in[p % SLOTS], 64 * (p // SLOTS + 1))
                pool.tensor_scalar(mask[:, p % 2], stage[:, p % SLOTS], 0.0, None, ALU.is_gt).then_inc(conv_done, 1)
            pool.wait_ge(pmax_ready, 1)
            pool.partition_all_reduce(all_max[:], part_max[:], P, RMAX).then_inc(amax_ready, 1)

            pool.wait_ge(mv1_ready, 1)
            pool.wait_ge(rs1_ready, 1)
            pool.wait_ge(f1_made, 2)
            pool.wait_ge(prod2_ready, 2)
            wide = lambda t: t.unsqueeze(2).to_broadcast([P, NK, D])
            pool.tensor_tensor(xin, x_j, wide(mv1[:, :, 0]), ALU.subtract).then_inc(xin_made, 1)
            pool.wait_ge(xin_made, 1)
            pool.tensor_tensor(xin, xin, wide(rs1[:]), ALU.mult).then_inc(xin_step, 1)
            pool.wait_ge(xin_step, 1)
            n, steps = NK // 2, 6
            while n:
                pool.tensor_tensor(xin[:, 0:n], xin[:, 0:n], xin[:, n:2 * n], ALU.add).then_inc(pool_step, 1)
                steps += 1
                pool.wait_ge(pool_step, steps)
                n //= 2
            pool.drain().then_inc(xin_sum, 1)

            splits = [0]

            def split(raw, hi, lo, arrived=None):
                if arrived is not None:
                    pool.wait_ge(*arrived)
                n, splits[0] = splits[0], splits[0] + 1
                pool.tensor_scalar(raw, raw, W_SCALE, None, ALU.mult).then_inc(w_step, 1)
                pool.wait_ge(w_step, 2 * n + 1)
                pool.tensor_copy(hi, raw).then_inc(w_step, 1)
                pool.wait_ge(w_step, 2 * n + 2)
                pool.tensor_tensor(lo, raw, hi, ALU.subtract).then_inc(wsplit, 1)

            pool.wait_ge(late_in, 16 * 9)
            split(gate_sb[:], gate_hl[:, 0:E], gate_hl[:, E:2 * E])
            pool.wait_ge(S_step, 1)
            pool.tensor_scalar(all_rows[:], all_rows[:], ident[:, D - 1:D], None, ALU.mult).then_inc(S_step, 1)
            pool.wait_ge(S_step, 2)
            pool.tensor_copy(all_h[:], all_rows[:]).then_inc(S_step, 1)
            pool.wait_ge(S_step, 3)
            pool.tensor_tensor(all_l[:], all_rows[:], all_h[:], ALU.subtract).then_inc(all_ready, 1)
            split(b2_sb[:], b2h[:], b2l[:])
            pool.wait_ge(wsplit, 2)
            pool.tensor_scalar(b2h[:], b2h[:], upper[:], None, ALU.mult).then_inc(S_step, 1)
            pool.tensor_scalar(b2l[:], b2l[:], lower[:], None, ALU.mult).then_inc(S_step, 1)
            pool.wait_ge(S_step, 5)
            pool.tensor_tensor(b2hl[:], b2l[:], b2h[:], ALU.add).then_inc(b2_split, 1)

            def post(s):
                own = x2[:, bass.ds(s * TS, TS), :]
                pool.tensor_copy(xown[:], own)
                pool.drain()
                pool.wait_ge(att_ready, s + 1)
                pool.tensor_tensor(xs[:], xn2[:], xown[:], ALU.add).then_inc(xs_ready, 1)
                pool.tensor_tensor(own, xn2[:], xown[:], ALU.add).then_inc(x2_kept, 1)
                pool.drain()

            pool.wait_ge(xn_in[0], 16)
            post(0)
            pool.wait_ge(xn_in[1], 16)
            post(1)
            post(2)
            split(w1raw, w1h[:], w1l[:], arrived=(w_in, 32))
            post(3)
            split(w2raw, w2h[:], w2l[:])
            with pool.Fori(4, NS - 1) as s:
                post(s)
            pool.wait_ge(xs_ready, NS)
            pool.tensor_copy(x2[:, (NS - 1) * TS:NS * TS, :], xs[:]).then_inc(x2_kept, 1)

        @block.scalar
        def _(act):
            small = [(W_sb[:], gnn_w), (w_col[:, 0:1], gnn_w1.rearrange("(p a) -> p a", a=1)),
                     (w_col[:, 1:2], gnn_w2.rearrange("(p a) -> p a", a=1)),
                     (b_col[:], gnn_b.rearrange("(p a) -> p a", a=1)),
                     (gb12[:, 0:1], gnn_b1.rearrange("(p a) -> p a", a=1).partition_broadcast(P)),
                     (gb12[:, 1:2], gnn_b2.rearrange("(p a) -> p a", a=1).partition_broadcast(P)),
                     (gate_sb[:], gate_w), (gateb_sb[:], gate_b.rearrange("(a e) -> a e", a=1).partition_broadcast(P)),
                     (b1_sb[:], b1.rearrange("e (c f) -> (e c) f", c=FC)),
                     *[(b2_sb[E * i:E * i + E], b2) for i in range(4)]]
            for n, (dst, src) in enumerate(small):
                if len(src.shape) == 3:
                    src = src.rearrange("p a e -> p (a e)")
                act.dma_start(dst, src).then_inc(small_in if n < 4 else late_in, 16)

            def convert(s, p):
                act.wait_ge(adj_in[p % SLOTS], 64 * (s * 2 + p // SLOTS + 1))
                need(act, turned, s * NP + p - 1)
                act.activation(mask[:, p % 2], stage[:, p % SLOTS], ACT.Sigmoid, bias=sig_bias[:],
                               scale=1000.0).then_inc(conv_done, 1)

            for n in range(2):
                act.wait_ge(prod2_ready, n + 1)
                for k in range(n * NK // 2, (n + 1) * NK // 2):
                    ins = act.activation(prod2[:, k], prod2[:, k], ACT.Copy, accum_out=f2_col[:, k:k + 1])
                ins.then_inc(f2_made, 1)
            act.wait_ge(dve_const, 1)
            act.wait_ge(bias_ready, 1)
            act.activation(r_col[:], f2_col[:], ACT.Exp, bias=bias_r[:], scale=-STEEP).then_inc(ru_exp, 1)
            act.activation(u_col[:], f2_col[:], ACT.Exp, bias=bias_u[:]).then_inc(ru_exp, 1)
            g_nat = g_row[:, :].rearrange("p (q b a e) -> p b q a e", q=Q, b=NB, a=32, e=4)
            for b in range(NB):
                act.wait_ge(f1row_ready, b + 1)
                act.activation(g_nat[:, b], bank[:, ROWS[b % len(ROWS)], :].rearrange("p (e q a) -> p q a e", e=4, q=Q),
                               ACT.Exp, bias=bias_g[:], scale=STEEP).then_inc(grow_ready, 1)
            act.wait_ge(mv1_ready, 1)
            act.activation(sd1[:], mv1[:, :, 1], ACT.Sqrt, bias=eps[:]).then_inc(sd1_ready, 1)
            act.wait_ge(b1_ready, 1)
            act.activation(b1T[:], bank[:, 3, 0:E * FC], ACT.Copy).then_inc(b1_copied, 1)

            def post_a(s, par):
                act.wait_ge(c_used, s * NK + NK)
                act.activation(oT[:], bank[:, par, :], ACT.Copy).then_inc(oT_copied, 1)

            def post_b(s):
                act.wait_ge(rinv_ready, s + 1)
                for t in range(TS):
                    ins = act.activation(xn2[:, t], sums[:, t // 2, t % 2, 0:D], ACT.Copy, scale=rinv[:, t:t + 1])
                ins.then_inc(att_ready, 1)

            def post_std(s):
                act.wait_ge(mv2_ready, s + 1)
                act.activation(sd2[:], mv2[:, :, 1], ACT.Sqrt, bias=eps[:]).then_inc(sd2_ready, 1)

            def post_c(s):
                if not (isinstance(s, int) and s == NS - 1):
                    act.wait_ge(x2_kept, s + 1)
                act.wait_ge(nmr_ready, s + 1)
                for t in range(TS):
                    ins = act.activation(xn2[:, t], xs[:, t], ACT.Identity, bias=nmr[:, t:t + 1], scale=rs2[:, t:t + 1])
                ins.then_inc(xn2_ready, 1)

            def post_d(s):
                act.wait_ge(xt_ready, s + 1)
                act.activation(xh[:, bass.ds(s * ST, ST)], bank[:, 5, :], ACT.Copy, scale=X_SCALE).then_inc(xh_ready, 1)

            def route_exp(n0, n1, r):
                act.wait_ge(lgd_ready, r + 1)
                act.activation(pr[:, n0:n1], lg[:, n0:n1], ACT.Exp).then_inc(pr_ready, 1)

            def route_copy(n0, n1, r):
                for g in (2,) if r else (0, 1):
                    rows = (GROUPS[g][1] - GROUPS[g][0]) * E
                    act.wait_ge(cwr_ready, 3 if r else 2)
                    act.activation(cwR[0:rows, g], bank[0:rows, 4, P * g:P * g + P], ACT.Copy).then_inc(cwr_copied, 1)
                for n in range(n0, n1, 8):
                    m = min(8, n1 - n)
                    src = bank[0:4 * E, 7 if r else BA[n // 8], 0:m * P // 2].bitcast(F16)
                    act.wait_ge(cwt_ready, n // 8 + 1)
                    act.activation(cwT[:, P * n:P * (n + m)], src, ACT.Copy).then_inc(cwt_copied, 1)

            def supertile(s, par, first=False, last=False):
                for p in range(NP):
                    if first:
                        for k in range(AHEAD + 4 * p, min(AHEAD + 4 * p + 4, NK)):
                            act.activation(Y[:, k, 0:D - 1], x_j[:, k, 0:D - 1], ACT.Identity, bias=nmru[:, k:k + 1],
                                           scale=ru[:, k:k + 1]).then_inc(y_rows, 1)
                    if not last:
                        convert(s + 1, p)
                    if p == 6 and first:
                        act.wait_ge(S_ready, 1)
                        act.activation(all_rows[:, 0:D], bank[:, 3, 0:D], ACT.Copy).then_inc(S_step, 1)
                    if p == 0 and not first:
                        post_a(s - 1, 1 - par)
                    if last and p == 0:
                        route_exp(*ROUTE[0])
                    if p == 2 and not first:
                        post_b(s - 1)
                    if p == 3 and not first:
                        post_std(s - 1)
                    if p == 4 and not first:
                        post_c(s - 1)
                    if p == 5 and not first:
                        post_d(s - 1)

            for p in range(NP):
                if p not in CONV_DVE + CONV_POOL:
                    act.wait_ge(conv_done, p)
                    convert(0, p)
            act.wait_ge(y_rows, AHEAD + 1)
            supertile(0, 0, first=True)
            with act.Fori(0, NS // 2 - 1) as i:
                supertile(i * 2 + 1, 1)
                supertile(i * 2 + 2, 0)
            supertile(NS - 1, 1, last=True)
            route_copy(*ROUTE[0])
            act.activation(warm[:], eps[:], ACT.Gelu)
            post_a(NS - 1, 1)

            def gelu(j, e):
                for f in range(FC):
                    act.wait_ge(h_ready, FC * j + f + 1)
                    if f == 0:
                        need(act, hw_done, j - 1)
                    act.activation(h[:, e % 2, f], bank[:, 2 * ((e + 1) % 2) + f, :], ACT.Gelu,
                                   bias=b1T[:, FC * e + f:FC * e + f + 1],
                                   scale=1.0 / (X_SCALE * W_SCALE)).then_inc(gelu_done, 1)

            def high(j, e):
                act.wait_ge(hw_done, j + 1)
                need(act, ffn2_done, j + 1 - HR)
                act.activation(hh[:, e % HR], hw[:, e % 2], ACT.Copy).then_inc(hh_done, 1)

            def copy_y(st):
                act.wait_ge(ffn2_done, (st + 1) * E)
                act.activation(y_sb, bank[:, 6, :], ACT.Copy, scale=1.0 / (C_SCALE * W_SCALE)).then_inc(y_copied, 1)

            def experts(st):
                for e in range(E):
                    now = (st, e) if isinstance(st, int) else None
                    if e == LAG and not (now and st == 0):
                        copy_y(st - 1)
                    gelu(st * E + e, e)
                    if now != (0, 0):
                        high(st * E + e - 1, (e - 1) % E)
                    if now == (0, 5):
                        post_std(NS - 1)
                    if now == (0, 7):
                        post_c(NS - 1)
                    if now == (1, 1):
                        post_d(NS - 1)
                    if now == (1, 6):
                        route_exp(*ROUTE[1])
                    if now == (2, 6):
                        route_copy(*ROUTE[1])

            for st in range(PEELED):
                experts(st)
            with act.Fori(PEELED, NS) as st:
                experts(st)
            high(NS * E - 1, E - 1)
            copy_y(NS - 1)

        @block.vector
        def _(dve):
            steps = [0, 0]

            def link(ins):
                steps[0] += 1
                ins.then_inc(dve_step, 1)
                dve.wait_ge(dve_step, steps[0])

            dve.memset(ones[:], 1.0)
            dve.memset(sig_bias[:], -500.0)
            link(dve.memset(eps[:], LN_EPS))
            dve.drain().then_inc(dve_const, 1)
            dve.wait_ge(small_in, 64)
            B1 = 5 * NK // 8
            dve.tensor_scalar(w_rep[:, 0], ones[:], w_col[:, 0:1], None, ALU.mult)
            dve.tensor_scalar(w_rep[:, 1], ones[:], w_col[:, 1:2], None, ALU.mult)
            dve.tensor_scalar(b_rep, ones[:], b_col[:], None, ALU.mult).then_inc(brep_done, 1)
            dve.wait_ge(gc_done, 1)
            dve.tensor_copy(G, bank[:, 4, 0:2 * D].rearrange("p (v d) -> p v d", v=2)).then_inc(g_copied, 1)
            dve.wait_ge(g_copied, 1)
            for n in range(2):
                part = slice(n * NK // 2, (n + 1) * NK // 2)
                dve.wait_ge(in2_in[n], 64)
                link(dve.tensor_tensor(prod1[:, part], in2_j[:, part], G[:, 0:1].to_broadcast([P, NK // 2, D]), ALU.mult))
                dve.tensor_reduce(f1_col[:, part], prod1[:, part], AX_X, ALU.add).then_inc(f1_made, 1)
            dve.wait_ge(late_in, 16 * 9)
            dve.tensor_tensor(c12[:], bank[:, 4, 2 * D:2 * D + 2], gb12[:], ALU.add)
            at = maskT[:].rearrange("p r s b i e -> p r s b e i")
            at32v = maskT[:].rearrange("p r s b i e -> p r s (b i e)").bitcast(U32)
            mask32 = mask[:].rearrange("p r s j -> p r (s j)").bitcast(U32)

            def turn(s, p, par):
                dve.wait_ge(conv_done, s * NP + p + 1)
                dve.transpose(at32v[:, par, PS_ * p:PS_ * p + PS_, :].rearrange("p s w -> p (s w)"),
                              mask32[:, p % 2]).then_inc(turned, 1)

            def convert(p):
                dve.wait_ge(adj_in[p % SLOTS], 64 * (p // SLOTS + 1))
                need(dve, turned, p - 1)
                dve.wait_ge(conv_done, p)
                dve.tensor_scalar(mask[:, p % 2], stage[:, p % SLOTS], 0.0, None, ALU.is_gt).then_inc(conv_done, 1)

            def stats(k0, k1):
                for k in range(k0, k1):
                    ins = dve.bn_stats(st1[:, k], x_j[:, k])
                return ins

            dve.wait_ge(xj_in, 64)
            stats(0, B1)
            dve.wait_ge(f1_made, 2)
            dve.wait_ge(f2_made, 2)
            link(dve.tensor_scalar(nf2[:], f2_col[:], -1.0, None, ALU.mult))
            dve.tensor_reduce(part_max[:, 0:1], f1_col[:], AX_X, ALU.max)
            dve.tensor_reduce(part_max[:, 1:2], f2_col[:], AX_X, ALU.max)
            dve.tensor_reduce(part_max[:, 2:3], nf2[:], AX_X, ALU.max).then_inc(pmax_ready, 1)
            convert(1)
            dve.wait_ge(amax_ready, 1)
            F1, F2, NF2 = all_max[:, 0:1], all_max[:, 1:2], all_max[:, 2:3]
            tt = lambda o, a, b, op: dve.tensor_tensor(o, a, b, op)
            link(tt(tmp[:, 0:1], c12[:, 0:1], c12[:, 1:2], ALU.add))
            tt(tmp[:, 1:2], tmp[:, 0:1], F2, ALU.add)
            link(tt(tmp[:, 2:3], F2, NF2, ALU.add))
            link(tt(tmp[:, 3:4], tmp[:, 1:2], F1, ALU.add))
            link(tt(tmp[:, 4:5], tmp[:, 3:4], tmp[:, 2:3], ALU.max))
            link(dve.tensor_scalar(tmp[:, 5:6], tmp[:, 4:5], STEEP, None, ALU.mult))
            dve.scalar_tensor_tensor(bias_g[:], tmp[:, 1:2], STEEP, tmp[:, 5:6], ALU.mult, ALU.subtract)
            dve.scalar_tensor_tensor(bias_r[:], F2, STEEP, tmp[:, 5:6], ALU.mult, ALU.subtract)
            dve.tensor_scalar(bias_u[:], F2, -1.0, None, ALU.mult).then_inc(bias_ready, 1)

            link(stats(B1, NK))
            for k in range(NK):
                ins = dve.bn_aggr(mv1[:, k], st1[:, k])
            ins.then_inc(mv1_ready, 1)
            turn(0, 0, 0)
            turn(0, 1, 0)
            for p in (2, 3):
                convert(p)
                turn(0, p, 0)
            dve.wait_ge(ru_exp, 2)
            dve.tensor_copy(Y[:, :, D - 1], u_col[:]).then_inc(y_rows, 1)
            dve.wait_ge(sd1_ready, 1)
            dve.reciprocal(rs1[:], sd1[:]).then_inc(rs1_ready, 1)
            dve.wait_ge(rs1_ready, 1)
            dve.wait_ge(mv1_ready, 1)
            link(dve.tensor_tensor(ru[:], rs1[:], u_col[:], ALU.mult))
            dve.scalar_tensor_tensor(nmru[:], mv1[:, :, 0], -1.0, ru[:], ALU.mult, ALU.mult)

            def row_chunk(k):
                dve.tensor_scalar(Y[:, k, 0:D - 1], x_j[:, k, 0:D - 1], mv1[:, k, 0:1], ru[:, k:k + 1],
                                  ALU.subtract, ALU.mult).then_inc(y_rows, 1)

            for k in range(AHEAD):
                row_chunk(k)
            for p in range(4, NP):
                if p in CONV_DVE:
                    convert(p)
                turn(0, p, 0)

            POST = 3

            def post_0(s):
                dve.wait_ge(oT_copied, s + 1)
                dve.tensor_scalar(empty[:], oT[:], 0.0, None, ALU.is_equal).then_inc(empty_ready, 1)

            def post_a(s):
                dve.wait_ge(n_ready, s + 1)
                dve.reciprocal(rinv[:].rearrange("p (b t) -> p b t", b=2), sums[:, :, :, D]).then_inc(rinv_ready, 1)

            def post_sum(s):
                dve.wait_ge(rinv_ready, s + 1)
                for t in range(TS):
                    ins = dve.scalar_tensor_tensor(xs[:, t], sums[:, t // 2, t % 2, 0:D], rinv[:, t:t + 1],
                                                   x2[:, s * TS + t], ALU.mult, ALU.add)
                ins.then_inc(xs_ready, 1)

            def post_b(s, n):
                if n == 0:
                    dve.wait_ge(xs_ready, s + 1)
                    for t in range(TS):
                        ins = dve.bn_stats(st2[:, t], xs[:, t])
                    ins.then_inc(post_step, 1)
                if n == 1:
                    for t in range(TS):
                        ins = dve.bn_aggr(mv2[:, t], st2[:, t])
                    ins.then_inc(mv2_ready, 1)
                if n == 2:
                    dve.wait_ge(sd2_ready, s + 1)
                    dve.reciprocal(rs2[:], sd2[:]).then_inc(post_step, 1)
                if n == 3:
                    dve.scalar_tensor_tensor(nmr[:], mv2[:, :, 0], -1.0, rs2[:], ALU.mult, ALU.mult).then_inc(nmr_ready, 1)

            def post_c(s):
                cols = bass.ds(s * ST, ST)
                dve.wait_ge(xh_ready, s + 1)
                dve.scalar_tensor_tensor(xl[:, cols], bank[:, 5, :], X_SCALE, xh[:, cols], ALU.mult,
                                         ALU.subtract).then_inc(xl_ready, 1)

            def post_d(s):
                halves = bank[:, 7, 0:2 * TS * E].rearrange("p (t v e) -> p t v e", v=2, e=E)
                dve.wait_ge(lgp_ready, s + 1)
                dve.scalar_tensor_tensor(lgl[:], halves[:, :, 1], 1.0 / (X_SCALE * W_SCALE),
                                         gateb_sb[:].unsqueeze(1).to_broadcast([P, TS, E]),
                                         ALU.mult, ALU.add).then_inc(post_step, 1)
                dve.wait_ge(post_step, s * POST + POST)
                dve.scalar_tensor_tensor(lg[:, bass.ds(s * TS, TS), :], halves[:, :, 0], 1.0 / (X_SCALE * W_SCALE),
                                         lgl[:], ALU.mult, ALU.add).then_inc(lg_kept, 1)

            def route_a(n0, n1, r):
                dve.wait_ge(lg_kept, NS - 2 * (1 - r))
                L = lg[:, n0:n1, :]
                link(dve.tensor_reduce(rowv[:, 0, n0:n1], L, AX_X, ALU.max))
                tt(L, L, rowv[:, 0, n0:n1].unsqueeze(2).to_broadcast([P, n1 - n0, E]), ALU.subtract).then_inc(lgd_ready, 1)

            def route_b(n0, n1, r):
                L, Pr, code_, s1, s2 = (t[:, n0:n1, :] for t in (lg, pr, code, sel1, sel2))
                row = lambda v: rowv[:, v, n0:n1]
                tok = lambda v: row(v).unsqueeze(2).to_broadcast([P, n1 - n0, E])

                def mark(ins):
                    steps[0] += 1
                    ins.then_inc(dve_step, 1)
                    return steps[0]

                dve.wait_ge(pr_ready, r + 1)
                dve.tensor_reduce(row(1), Pr, AX_X, ALU.add)
                done = mark(dve.tensor_reduce(row(2), Pr, AX_X, ALU.max))
                for chosen, t in ((s1, Pr), (s2, L)):
                    yield
                    dve.wait_ge(dve_step, done)
                    done = mark(tt(code_, t, tok(2), ALU.is_equal))
                    yield
                    dve.wait_ge(dve_step, done)
                    done = mark(tt(code_, code_, order[:].unsqueeze(1).to_broadcast([P, n1 - n0, E]), ALU.mult))
                    yield
                    dve.wait_ge(dve_step, done)
                    done = mark(dve.tensor_reduce(row(3), code_, AX_X, ALU.max))
                    yield
                    dve.wait_ge(dve_step, done)
                    done = mark(tt(chosen, code_, tok(3), ALU.is_equal))
                    if chosen is s1:
                        yield
                        dve.wait_ge(dve_step, done)
                        done = mark(dve.scalar_tensor_tensor(L, s1, -2.0, Pr, ALU.mult, ALU.add))
                        yield
                        dve.wait_ge(dve_step, done)
                        done = mark(dve.tensor_reduce(row(2), L, AX_X, ALU.max))
                yield
                dve.wait_ge(dve_step, done)
                dve.reciprocal(row(0), row(1))
                done = mark(tt(s1, s1, s2, ALU.add))
                yield
                dve.wait_ge(dve_step, done)
                done = mark(tt(Pr, Pr, s1, ALU.mult))
                yield
                dve.wait_ge(dve_step, done)
                done = mark(dve.scalar_tensor_tensor(Pr, Pr, C_SCALE, tok(0), ALU.mult, ALU.mult))
                yield
                dve.wait_ge(dve_step, done)
                twice = Pr.unsqueeze(2).to_broadcast([P, n1 - n0, 2, E])
                done = mark(dve.tensor_copy(cw16[:, n0:n1, :, 0], twice))
                yield
                dve.wait_ge(dve_step, done)
                tt(cw16[:, n0:n1, :, 1], twice, cw16[:, n0:n1, :, 0], ALU.subtract).then_inc(cw_ready, 1)


            BN = (12, 13, 17, 18)

            def supertile(s, par, first=False, last=False):
                router = route_b(*ROUTE[0])
                for k in range(NK):
                    if k == 0:
                        dve.wait_ge(turned, (s + 1) * NP)
                    if first and k == 0:
                        dve.wait_ge(grow_ready, NB)
                    need(dve, c_used, s * NK + k - CR + 1)
                    if not first and k in (BN[1], BN[3]):
                        dve.wait_ge(post_step, (s - 1) * POST + (1 if k == BN[1] else 2))
                    dve.scalar_tensor_tensor(
                        c[:, k % CR].rearrange("p (s i) -> p s i", i=32),
                        g_row[:, bass.ds(s * ST, ST)].rearrange("p (s i) -> p s i", i=32), r_col[:, k:k + 1],
                        at[:, par, :, k // 4, k % 4, :], ALU.max, ALU.mult).then_inc(c_ready, 1)
                    if k % 4 == 3 and not last:
                        turn(s + 1, k // 4, 1 - par)
                    if not first and k == 5:
                        post_0(s - 1)
                    if not first and k == 8:
                        post_a(s - 1)
                    if not first and k in BN:
                        post_b(s - 1, BN.index(k))
                    if not first and k == 25:
                        post_c(s - 1)
                    if not first and k == 30:
                        post_d(s - 1)
                    if last and k == 3:
                        route_a(*ROUTE[0])
                    if last and k >= 9:
                        next(router, None)
            supertile(0, 0, first=True)
            with dve.Fori(0, NS // 2 - 1) as i:
                supertile(i * 2 + 1, 1)
                supertile(i * 2 + 2, 0)
            supertile(NS - 1, 1, last=True)

            def weigh(j, e, st):
                dve.wait_ge(gelu_done, FC * (j + 1))
                if e % (E // 2) == 0:
                    dve.wait_ge(wb_in[e // (E // 2)], 16 * (st + 1))
                need(dve, hl_done, j - 1)
                dve.tensor_tensor(hw[:, e % 2], h[:, e % 2], wb[:, e].unsqueeze(1).to_broadcast([P, FC, ST]),
                                  ALU.mult).then_inc(hw_done, 1)

            def low(j, e):
                dve.wait_ge(hh_done, j + 1)
                need(dve, ffn2_done, j + 1 - HR)
                dve.tensor_tensor(hl[:, e % HR], hw[:, e % 2], hh[:, e % HR], ALU.subtract).then_inc(hl_done, 1)

            def add_out(st):
                dve.wait_ge(yt_ready, st + 1)
                dve.wait_ge(out_free, st * 16 + 1)
                dve.tensor_tensor(out_sb, bank[:, 5, :].rearrange("p (t d) -> p t d", d=D),
                                  x2[:, bass.ds(st * TS, TS), :], ALU.add).then_inc(out_added, 1)

            dve.memset(tmp[:, 7:8], 0.0).then_inc(out_free, 1)
            router = route_b(*ROUTE[1])

            def experts(st):
                for e in range(E):
                    now = (st, e) if isinstance(st, int) else None
                    if now == (0, 0):
                        post_0(NS - 1)
                    if now == (0, 1):
                        post_a(NS - 1)
                        post_sum(NS - 1)
                    routing = now and (1, 7) <= now <= (2, 4)
                    if routing:
                        next(router, None)
                    weigh(st * E + e, e, st)
                    if routing:
                        next(router, None)
                    if now != (0, 0):
                        low(st * E + e - 1, (e - 1) % E)
                    if e == LAG + 1 and not (now and st == 0):
                        add_out(st - 1)
                    if now == (0, 3):
                        post_b(NS - 1, 0)
                    if now == (0, 4):
                        dve.wait_ge(post_step, (NS - 1) * POST + 1)
                        post_b(NS - 1, 1)
                    if now == (0, 6):
                        post_b(NS - 1, 2)
                        dve.wait_ge(post_step, (NS - 1) * POST + 2)
                        post_b(NS - 1, 3)
                    if now == (1, 2):
                        post_c(NS - 1)
                    if now == (1, 4):
                        post_d(NS - 1)
                        dve.wait_ge(x2_kept, NS)
                    if now == (1, 5):
                        route_a(*ROUTE[1])
                    if routing:
                        next(router, None)

            for st in range(PEELED):
                experts(st)
            with dve.Fori(PEELED, NS) as st:
                experts(st)
            low(NS * E - 1, E - 1)
            add_out(NS - 1)

        @block.tensor
        def _(pe):
            mm = pe.matmul
            pe.wait_ge(brep_done, 1)
            for v in range(2):
                mm(bank[:, 4, D * v:D * v + D], w_rep[:, v], W_sb[:], start=True, stop=True)
            mm(bank[:, 4, 2 * D:2 * D + 2], b_rep, w_col[:], start=True, stop=True).then_inc(gc_done, 1)
            pe.wait_ge(pool_const, 1)
            pe.wait_ge(late_in, 16 * 9)
            pe.transpose(bank[:, 3, 0:E * FC], b1_sb[:], ident[0:E * FC, 0:E * FC]).then_inc(b1_ready, 1)
            for b in range(NB):
                pe.wait_ge(f1_made, 1 if b < NB // 2 else 2)
                need(pe, grow_ready, b - len(ROWS) + 1)
                for e in range(4):
                    k = 4 * b + e
                    ins = mm(bank[:, ROWS[b % len(ROWS)], P * e:P * e + P], f1_col[:, k:k + 1].to_broadcast([P, P]),
                             ident[:], start=True, stop=True)
                ins.then_inc(f1row_ready, 1)

            def post_a(s):
                pe.wait_ge(all_ready, 1)
                pe.wait_ge(oT_copied, s + 1)
                for t in range(TS):
                    mm(sums[:, t // 2, t % 2, 0:D + 1], oT[:, P * t:P * t + P], back[:, 0:D + 1], start=True, stop=False)
                    if t == 0:
                        pe.wait_ge(empty_ready, s + 1)
                    mm(sums[:, t // 2, t % 2, 0:D + 1], empty[:, P * t:P * t + P], all_h[:], start=False, stop=False)
                    ins = mm(sums[:, t // 2, t % 2, 0:D + 1], empty[:, P * t:P * t + P], all_l[:], start=False, stop=True)
                ins.then_inc(n_ready, 1)

            def post_b(s):
                pe.wait_ge(xn2_ready, s + 1)
                for t in range(TS):
                    ins = pe.transpose(bank[:, 5, P * t:P * t + P], xn2[:, t], ident[:])
                ins.then_inc(xt_ready, 1)

            def post_c(s):
                pe.wait_ge(wsplit, 1)
                pe.wait_ge(xl_ready, s + 1)
                for t in range(TS):
                    toks = bass.ds(s * ST + P * t, P)
                    dst = bank[:, 7, 2 * E * t:2 * E * t + 2 * E]
                    mm(dst, xh[:, toks], gate_hl[:], start=True, stop=False)
                    ins = mm(dst[:, 0:E], xl[:, toks], gate_hl[:, 0:E], start=False, stop=True)
                ins.then_inc(lgp_ready, 1)

            def route(n0, n1, r):
                pe.wait_ge(cw_ready, r + 1)
                for g in (2,) if r else (0, 1):
                    a, b = GROUPS[g]
                    pe.transpose(bank[0:(b - a) * E, 4, P * g:P * g + P],
                                 pr[:, a:b, :].rearrange("p n e -> p (n e)"), ident[:]).then_inc(cwr_ready, 1)
                for n in range(n0, n1, 8):
                    m = min(8, n1 - n)
                    dst = bank[0:4 * E, 7 if r else BA[n // 8], :].bitcast(F16)
                    for t in range(m):
                        ins = pe.transpose(dst[:, P * t:P * t + P], cw16[:, n + t].rearrange("p r v e -> p (r v e)"),
                                           ident16[:])
                    ins.then_inc(cwt_ready, 1)

            def supertile(s, par, first=False, last=False):
                for k in range(NK):
                    if first:
                        pe.wait_ge(y_rows, k + 2)
                    pe.wait_ge(c_ready, s * NK + k + 1)
                    mm(bank[:, par, :], Y[:, k], c[:, k % CR], start=(k == 0), stop=(k == NK - 1)).then_inc(c_used, 1)
                    if first and k == NK - 12:
                        pe.wait_ge(xin_sum, 1)
                        mm(bank[:, 3, 0:D], ones[:], xin[:, 0], start=True, stop=True).then_inc(S_ready, 1)
                    if not first and k == 4:
                        post_a(s - 1)
                    if not first and k == 19:
                        post_b(s - 1)
                    if not first and k == 24:
                        post_c(s - 1)
                    if last and k == 25:
                        route(*ROUTE[0])

            pe.wait_ge(b1_copied, 1)
            pe.wait_ge(grow_ready, NB)
            pe.wait_ge(conv_done, NP - 1)
            for _ in range(WARM):
                mm(bank[:, 3, 0:P], ones[:], ident[:], start=True, stop=True)
            supertile(0, 0, first=True)
            with pe.Fori(0, NS // 2 - 1) as i:
                supertile(i * 2 + 1, 1)
                supertile(i * 2 + 2, 0)
            supertile(NS - 1, 1, last=True)
            pe.wait_ge(wsplit, 4)
            pe.wait_ge(b2_split, 1)

            def ffn1(j, e, st):
                cols = bass.ds(st * ST, ST)
                need(pe, gelu_done, FC * (j - 1))
                for f in range(FC):
                    wh, wl = w1h[:, e, P * f:P * f + P], w1l[:, e, P * f:P * f + P]
                    dst = bank[:, 2 * ((e + 1) % 2) + f, :]
                    mm(dst, wh, xh[:, cols], start=True, stop=False)
                    mm(dst, wh, xl[:, cols], start=False, stop=False)
                    mm(dst, wl, xh[:, cols], start=False, stop=True).then_inc(h_ready, 1)

            def ffn2(j, e, st):
                dst = bank[:, 6, :]
                if e == 0:
                    need(pe, y_copied, st)
                pe.wait_ge(hl_done, j + 1)
                for f in range(FC):
                    wh, wl, r = w2h[:, FC * e + f], w2l[:, FC * e + f], e % HR
                    mm(dst, wh, hh[:, r, f], start=(e == 0 and f == 0), stop=False)
                    mm(dst, wh, hl[:, r, f], start=False, stop=False)
                    ins = mm(dst, wl, hh[:, r, f], start=False, stop=(e == E - 1 and f == FC - 1))
                ins.then_inc(ffn2_done, 1)
                if e == 0:
                    mm(dst, b2hl[:], cwT[:, bass.ds(st * ST, ST)], start=False, stop=False)

            def turn_y(st):
                pe.wait_ge(y_copied, st + 1)
                for t in range(TS):
                    ins = pe.transpose(bank[:, 5, P * t:P * t + P], y_sb[:, P * t:P * t + P], ident[:])
                ins.then_inc(yt_ready, 1)

            def experts(st):
                for e in range(E):
                    now = (st, e) if isinstance(st, int) else None
                    if now == (0, 0):
                        pe.wait_ge(cwt_copied, len(BA))
                    if now == (0, 1):
                        post_a(NS - 1)
                    ffn1(st * E + e, e, st)
                    if e >= LAG:
                        ffn2(st * E + e - LAG, e - LAG, st)
                    elif not (now and st == 0):
                        ffn2(st * E + e - LAG, e - LAG + E, st - 1)
                    if now == (1, 0):
                        post_b(NS - 1)
                    if now == (1, 3):
                        post_c(NS - 1)
                    if e == LAG and not (now and st == 0):
                        turn_y(st - 1)
                    if now == (2, 5):
                        route(*ROUTE[1])

            for st in range(PEELED):
                experts(st)
            with pe.Fori(PEELED, NS) as st:
                experts(st)
            for e in range(E - LAG, E):
                ffn2((NS - 1) * E + e, e, NS - 1)
            turn_y(NS - 1)


_INS = ["x", "adj", "L0_gnn_inlayer2", "L0_gnn_W", "L0_gnn_b", "L0_gnn_w1", "L0_gnn_b1", "L0_gnn_w2", "L0_gnn_b2",
        "L0_ffn_gate_w", "L0_ffn_gate_b", "L0_ffn_W1", "L0_ffn_b1", "L0_ffn_W2", "L0_ffn_b2"]


def kernel(**inputs):
    import numpy as np
    import concourse.bacc as bacc
    from concourse.bass_utils import run_bass_kernel_spmd

    nc = bacc.Bacc("TRN2", target_bir_lowering=False, num_devices=1)
    arrays, args = {}, []
    for name in _INS:
        a = np.ascontiguousarray(inputs[name])
        arrays[f"in_{name}"] = a
        args.append(nc.dram_tensor(f"in_{name}", a.shape, mybir.dt.from_np(a.dtype), kind="ExternalInput").ap())
    shares = nc.dram_tensor("shares", (inputs["L0_ffn_W1"].shape[0], inputs["x"].shape[0]), F32, kind="Internal").ap()
    out = nc.dram_tensor("out", inputs["x"].shape, F32, kind="ExternalOutput").ap()
    gnn_moe_kernel(nc, *args, shares, out)
    r = run_bass_kernel_spmd(nc, [arrays], core_ids=[0])
    return r.results[0]["out"]
```
